# Optimizing a Trainium2 kernel written in Bass

```python
import numpy as np
import jax
import jax.numpy as jnp

def _softmax(x, axis=-1):
    return jax.nn.softmax(x, axis=axis)

def _gelu(x):
    return jax.nn.gelu(x, approximate=True)

def _silu(x):
    return jax.nn.silu(x)

def _sigmoid(x):
    return jax.nn.sigmoid(x)

def _layernorm(x, axis=-1, eps=1e-05):
    m = jnp.mean(x, axis=axis, keepdims=True)
    v = jnp.var(x, axis=axis, keepdims=True)
    return (x - m) / jnp.sqrt(v + eps)

def _scatter_add(tgt, idx, src, axis=0):
    return tgt.at[idx].add(src)

def _segment_sum(src, seg, n):
    return jax.ops.segment_sum(src, seg, n)
kernel_name = 'mk_rec_standalone_d1_rec_r8_6c65bb'

def setup_inputs(seed: int=0):
    np.random.seed(seed)
    _w = jnp.asarray

    def _rec_inputs():
        import jax
        import jax.numpy as jnp
        _rk = jax.random.key(seed)
        r_dense_x = -0.00338568 + 1.0005 * jax.random.normal(jax.random.fold_in(_rk, 1), (512, 13), jnp.float32)
        r_cat_idx = jnp.stack([jax.random.randint(jax.random.fold_in(jax.random.fold_in(_rk, 2), 0), (512,), 2, 12500, jnp.int32), jax.random.randint(jax.random.fold_in(jax.random.fold_in(_rk, 2), 1), (512,), 1, 99999, jnp.int32), jax.random.randint(jax.random.fold_in(jax.random.fold_in(_rk, 2), 2), (512,), 0, 12500, jnp.int32), jax.random.randint(jax.random.fold_in(jax.random.fold_in(_rk, 2), 3), (512,), 5, 12500, jnp.int32), jax.random.randint(jax.random.fold_in(jax.random.fold_in(_rk, 2), 4), (512,), 20, 99993, jnp.int32), jax.random.randint(jax.random.fold_in(jax.random.fold_in(_rk, 2), 5), (512,), 0, 99993, jnp.int32), jax.random.randint(jax.random.fold_in(jax.random.fold_in(_rk, 2), 6), (512,), 2, 99999, jnp.int32), jax.random.randint(jax.random.fold_in(jax.random.fold_in(_rk, 2), 7), (512,), 2, 99995, jnp.int32), jax.random.randint(jax.random.fold_in(jax.random.fold_in(_rk, 2), 8), (512,), 0, 99999, jnp.int32), jax.random.randint(jax.random.fold_in(jax.random.fold_in(_rk, 2), 9), (512,), 2, 99986, jnp.int32), jax.random.randint(jax.random.fold_in(jax.random.fold_in(_rk, 2), 10), (512,), 4, 99999, jnp.int32), jax.random.randint(jax.random.fold_in(jax.random.fold_in(_rk, 2), 11), (512,), 15, 99999, jnp.int32), jax.random.randint(jax.random.fold_in(jax.random.fold_in(_rk, 2), 12), (512,), 0, 99989, jnp.int32), jax.random.randint(jax.random.fold_in(jax.random.fold_in(_rk, 2), 13), (512,), 5, 99990, jnp.int32), jax.random.randint(jax.random.fold_in(jax.random.fold_in(_rk, 2), 14), (512,), 2, 99996, jnp.int32), jax.random.randint(jax.random.fold_in(jax.random.fold_in(_rk, 2), 15), (512,), 3, 99994, jnp.int32), jax.random.randint(jax.random.fold_in(jax.random.fold_in(_rk, 2), 16), (512,), 0, 99998, jnp.int32), jax.random.randint(jax.random.fold_in(jax.random.fold_in(_rk, 2), 17), (512,), 13, 99998, jnp.int32), jax.random.randint(jax.random.fold_in(jax.random.fold_in(_rk, 2), 18), (512,), 10, 12498, jnp.int32), jax.random.randint(jax.random.fold_in(jax.random.fold_in(_rk, 2), 19), (512,), 0, 99999, jnp.int32), jax.random.randint(jax.random.fold_in(jax.random.fold_in(_rk, 2), 20), (512,), 0, 99995, jnp.int32), jax.random.randint(jax.random.fold_in(jax.random.fold_in(_rk, 2), 21), (512,), 1, 99998, jnp.int32), jax.random.randint(jax.random.fold_in(jax.random.fold_in(_rk, 2), 22), (512,), 1, 99997, jnp.int32), jax.random.randint(jax.random.fold_in(jax.random.fold_in(_rk, 2), 23), (512,), 2, 99989, jnp.int32), jax.random.randint(jax.random.fold_in(jax.random.fold_in(_rk, 2), 24), (512,), 6, 12500, jnp.int32), jax.random.randint(jax.random.fold_in(jax.random.fold_in(_rk, 2), 25), (512,), 2, 99995, jnp.int32)], axis=1)
        return (r_dense_x, r_cat_idx)
    r_dense_x, r_cat_idx = _rec_inputs()

    def _L0_rec_setup():
        import jax, jax.numpy as jnp
        import numpy as np
        N_CAT, N_CONT, E, VOCAB = (26, 13, 128, 12500)
        B = 2048
        DENSE_DIMS = [512, 256]
        TOP_DIMS = [1024, 1024, 512, 256]
        N_PAIRS = (N_CAT + 1) * N_CAT // 2
        TOP_IN = N_PAIRS + E

        def _dense_params(key, dims):
            Ws, bs, ks = ([], [], jax.random.split(key, len(dims) - 1))
            for i, k in enumerate(ks):
                fan_in, fan_out = (dims[i], dims[i + 1])
                Ws.append(jax.random.normal(k, (fan_in, fan_out), jnp.float32) / np.sqrt(fan_in).astype(np.float32))
                bs.append(jnp.zeros((fan_out,), jnp.float32))
            return (Ws, bs)
        key = jax.random.key(seed)
        k_x, k_i, k_e, k_b, k_t = jax.random.split(key, 5)
        dense_x = jax.random.normal(k_x, (B, N_CONT), jnp.float32)
        cat_idx = jax.random.randint(k_i, (B, N_CAT), 0, VOCAB, jnp.int64)
        emb_table = jax.random.normal(k_e, (N_CAT, VOCAB, E), jnp.float32) * 0.01
        (Wd1, Wd2, Wdf), (bd1, bd2, bdf) = _dense_params(k_b, [N_CONT] + DENSE_DIMS + [E])
        (Wt1, Wt2, Wt3, Wt4, Wo), (bt1, bt2, bt3, bt4, bo) = _dense_params(k_t, [TOP_IN] + TOP_DIMS + [1])
        return dict(dense_x=dense_x, cat_idx=cat_idx, emb_table=emb_table, Wd1=Wd1, bd1=bd1, Wd2=Wd2, bd2=bd2, Wdf=Wdf, bdf=bdf, Wt1=Wt1, bt1=bt1, Wt2=Wt2, bt2=bt2, Wt3=Wt3, bt3=bt3, Wt4=Wt4, bt4=bt4, Wo=Wo, bo=bo)
    _L0_rec_all = _L0_rec_setup()
    _L0_rec_in = {k: v for k, v in _L0_rec_all.items() if k in ('emb_table', 'Wd1', 'bd1', 'Wd2', 'bd2', 'Wdf', 'bdf', 'Wt1', 'bt1', 'Wt2', 'bt2', 'Wt3', 'bt3', 'Wt4', 'bt4', 'Wo', 'bo')}
    del _L0_rec_all
    return {'r_dense_x': r_dense_x, 'r_cat_idx': r_cat_idx, 'L0_rec_emb_table': _L0_rec_in['emb_table'], 'L0_rec_Wd1': _L0_rec_in['Wd1'], 'L0_rec_bd1': _L0_rec_in['bd1'], 'L0_rec_Wd2': _L0_rec_in['Wd2'], 'L0_rec_bd2': _L0_rec_in['bd2'], 'L0_rec_Wdf': _L0_rec_in['Wdf'], 'L0_rec_bdf': _L0_rec_in['bdf'], 'L0_rec_Wt1': _L0_rec_in['Wt1'], 'L0_rec_bt1': _L0_rec_in['bt1'], 'L0_rec_Wt2': _L0_rec_in['Wt2'], 'L0_rec_bt2': _L0_rec_in['bt2'], 'L0_rec_Wt3': _L0_rec_in['Wt3'], 'L0_rec_bt3': _L0_rec_in['bt3'], 'L0_rec_Wt4': _L0_rec_in['Wt4'], 'L0_rec_bt4': _L0_rec_in['bt4'], 'L0_rec_Wo': _L0_rec_in['Wo'], 'L0_rec_bo': _L0_rec_in['bo']}

def reference(r_dense_x, r_cat_idx, L0_rec_emb_table, L0_rec_Wd1, L0_rec_bd1, L0_rec_Wd2, L0_rec_bd2, L0_rec_Wdf, L0_rec_bdf, L0_rec_Wt1, L0_rec_bt1, L0_rec_Wt2, L0_rec_bt2, L0_rec_Wt3, L0_rec_bt3, L0_rec_Wt4, L0_rec_bt4, L0_rec_Wo, L0_rec_bo):
    import jax
    import jax.numpy as jnp

    def _L0_rec_ref(dense_x, cat_idx, emb_table, Wd1, bd1, Wd2, bd2, Wdf, bdf, Wt1, bt1, Wt2, bt2, Wt3, bt3, Wt4, bt4, Wo, bo):
        import jax, jax.numpy as jnp
        import numpy as np
        N_CAT, N_CONT, E, VOCAB = (26, 13, 128, 12500)
        B = 2048
        DENSE_DIMS = [512, 256]
        TOP_DIMS = [1024, 1024, 512, 256]
        N_PAIRS = (N_CAT + 1) * N_CAT // 2
        TOP_IN = N_PAIRS + E

        def _dense_params(key, dims):
            Ws, bs, ks = ([], [], jax.random.split(key, len(dims) - 1))
            for i, k in enumerate(ks):
                fan_in, fan_out = (dims[i], dims[i + 1])
                Ws.append(jax.random.normal(k, (fan_in, fan_out), jnp.float32) / np.sqrt(fan_in).astype(np.float32))
                bs.append(jnp.zeros((fan_out,), jnp.float32))
            return (Ws, bs)
        fm = emb_table[jnp.arange(N_CAT)[None, :], cat_idx]
        h = jax.nn.relu(dense_x @ Wd1 + bd1)
        h = jax.nn.relu(h @ Wd2 + bd2)
        dense = jax.nn.relu(h @ Wdf + bdf)
        Z = jnp.concatenate([fm, dense[:, None, :]], axis=1)
        S = jnp.einsum('bie,bje->bij', Z, Z)
        iu, ju = np.triu_indices(N_CAT + 1, k=1)
        interactions = S[:, iu, ju]
        x = jnp.concatenate([interactions, dense], axis=-1)
        x = jax.nn.relu(x @ Wt1 + bt1)
        x = jax.nn.relu(x @ Wt2 + bt2)
        x = jax.nn.relu(x @ Wt3 + bt3)
        x = jax.nn.relu(x @ Wt4 + bt4)
        return jax.nn.sigmoid(x @ Wo + bo)
    y = _L0_rec_ref(r_dense_x, r_cat_idx, L0_rec_emb_table, L0_rec_Wd1, L0_rec_bd1, L0_rec_Wd2, L0_rec_bd2, L0_rec_Wdf, L0_rec_bdf, L0_rec_Wt1, L0_rec_bt1, L0_rec_Wt2, L0_rec_bt2, L0_rec_Wt3, L0_rec_bt3, L0_rec_Wt4, L0_rec_bt4, L0_rec_Wo, L0_rec_bo)
    return y

_drawn_inputs = setup_inputs


def setup_inputs(seed=0):
    import zlib

    import numpy as np

    out = dict(_drawn_inputs(seed))
    spreads = {'L0_rec_bd1': (0.0, 0.8),
     'L0_rec_bd2': (0.0, 0.8),
     'L0_rec_bdf': (0.0, 0.8),
     'L0_rec_bt1': (0.0, 0.731),
     'L0_rec_bt2': (0.0, 0.285),
     'L0_rec_bt3': (0.0, 0.524),
     'L0_rec_bt4': (0.0, 0.8)}
    factors = {'r_dense_x': 4.758,
     'L0_rec_emb_table': 8.0,
     'L0_rec_Wd1': 5.207,
     'L0_rec_Wd2': 5.439,
     'L0_rec_Wdf': 3.865,
     'L0_rec_Wt1': 4.142,
     'L0_rec_Wt2': 2.74,
     'L0_rec_Wt3': 4.233,
     'L0_rec_Wt4': 3.12,
     'L0_rec_Wo': 4.006}
    for name, (base, spread) in spreads.items():
        noise = np.random.default_rng([zlib.crc32(name.encode()), seed]).standard_normal(out[name].shape)
        drawn = base * np.exp(spread * noise) if base else spread * noise
        out[name] = jnp.asarray(drawn.astype(out[name].dtype))
    for name, factor in factors.items():
        out[name] = (out[name] * factor).astype(out[name].dtype)
    return out
```

```python
import concourse.bass as bass
from concourse import mybir
from contextlib import ExitStack

F32 = mybir.dt.float32
F32R = mybir.dt.float32r
I32 = mybir.dt.int32
U32 = mybir.dt.uint32
ALU = mybir.AluOpType
ACT = mybir.ActivationFunctionType

P = 128
N_CAT, N_CONT, E, VOCAB = 26, 13, 128, 12500
BATCH = 512
TILES = BATCH // P
NZ = N_CAT + 1
HALF = NZ // 2
PAIRS = NZ * HALF
PAIR_CHUNKS = 3
IC = NZ // PAIR_CHUNKS
PC = IC * HALF
Q = 4
GROUPS = P // Q
ROUND = 8
ROUNDS = GROUPS // ROUND
ZG = 4
Z_GROUPS = [(f, min(ZG, N_CAT - f)) for f in range(0, N_CAT, ZG)]
NG = len(Z_GROUPS)
BOT = [N_CONT, 512, 256, E]
TOP = [PAIRS + E, 1024, 1024, 512, 256]
M1, M2, M3, M4 = (n // P for n in TOP[1:])
CH = M1 + M2 + M3 + M4 + 1
STAGES = 4
SPLIT_LOADS = M1 + M2 // 2

COLS = {}
_at = 0
for _name, _n in (("bd1", 4), ("bd2", 2), ("bdf", 1), ("bt1", M1), ("bt2", M2), ("bt3", M3), ("bt4", M4), ("Wo", M4)):
    COLS[_name] = _at
    _at += _n
N_SMALL = _at


def at_least(engine, sem, n):
    if n > 0:
        engine.wait_ge(sem, n)


def build(nc, x_t, cat_idx, emb, small, bo, wd1, wd2, wdf, wt1, wt2, wt3, wt4, out):
    ctx = ExitStack()
    with ctx:
        def sb(name, shape, dt=F32, where=ctx):
            return where.enter_context(nc.sbuf_tensor(name, shape, dt))

        def pb(name, shape, dt=F32):
            return ctx.enter_context(nc.psum_tensor(name, shape, dt))

        def sem(name):
            return ctx.enter_context(nc.semaphore(name))

        w1 = sb("w1", [P, 4, TOP[1]])
        w2h = sb("w2h", [P, M1, TOP[2]], F32R)
        w2l = sb("w2l", [P, M1, TOP[2]], F32R)
        w3h = sb("w3h", [P, M2, TOP[3]], F32R)
        w3l = sb("w3l", [P, M2, TOP[3]], F32R)
        w4 = sb("w4", [P, M3, TOP[4]])
        sm = sb("sm", [P, N_SMALL])
        bo_sb = sb("bo_sb", [1, 1])
        rows = [sb(f"rows{h}", [P, N_CAT, E]) for h in range(2)]
        zt = sb("zt", [P, GROUPS, Q, 32])
        s_ij = sb("s_ij", [P, NZ, GROUPS])
        xb = sb("xb", [P, NZ + HALF, 32])
        xp = sb("xp", [P, NZ, HALF])
        xt = sb("xt", [P, PAIR_CHUNKS, P])
        dense_t = sb("dense_t", [P, BATCH])
        ident = sb("ident", [P, P])
        idx = sb("idx", [P, TILES, N_CAT], I32)
        idx_neg = sb("idx_neg", [P, TILES, N_CAT], I32)
        idx_clip = sb("idx_clip", [P, TILES, N_CAT], I32)
        idx_wrap = sb("idx_wrap", [P, TILES, N_CAT], I32)
        row_of = sb("row_of", [P, TILES, N_CAT], I32)
        base = sb("base", [P, TILES, N_CAT], I32)
        act = sb("act", [P, 4, P])
        a3 = sb("a3", [P, M3, P])
        a4 = sb("a4", [P, M4, P])
        logits = sb("logits", [1, BATCH])

        with ExitStack() as early:
            xc = sb("xc", [N_CONT, BATCH], where=early)
            wd1_sb = sb("wd1_sb", [N_CONT, BOT[1]], where=early)
            wd2_sb = sb("wd2_sb", [P, 4, BOT[2]], where=early)
            wdf_sb = sb("wdf_sb", [P, 2, BOT[3]], where=early)
            h1 = sb("h1", [P, 4, BATCH], where=early)
            h2 = sb("h2", [P, 2, BATCH], where=early)
            stage01 = sb("stage01", [P, 1, 1024], where=early)
        a1h = sb("a1h", [P, M1, P], F32R)
        a1l = sb("a1l", [P, M1, P], F32R)
        a2h = sb("a2h", [P, M2, P], F32R)
        a2l = sb("a2l", [P, M2, P], F32R)
        stage = [rows[1][:, 8 * i:8 * i + 8, :].rearrange("p f e -> p (f e)") for i in range(3)]
        stage += [stage01[:, i, :] for i in range(1)]

        tp = pb("tp", [P, 2, 512])
        gp = pb("gp", [P, 4, 512])
        mp = pb("mp", [P, 2, 512])

        idx_in = sem("idx_in")
        small_in = sem("small_in")
        bottom_in = sem("bottom_in")
        wd2_in = sem("wd2_in")
        w1_in = sem("w1_in")
        w4_in = sem("w4_in")
        stage_in = [sem(f"stage_in{i}") for i in range(STAGES)]
        base_made = sem("base_made")
        ident_made = sem("ident_made")
        zt_zeroed = sem("zt_zeroed")
        idx_step = sem("idx_step")
        gathered = [[sem(f"gathered{h}_{g}") for g in range(NG)] for h in range(2)]
        bot_ready = sem("bot_ready")
        bot_out = sem("bot_out")
        w_hi = sem("w_hi")
        w_lo = sem("w_lo")
        tp_ready = sem("tp_ready")
        zt_act = sem("zt_act")
        zt_dve = sem("zt_dve")
        gram_ready = sem("gram_ready")
        ex_act = sem("ex_act")
        ex_dve = sem("ex_dve")
        xb_ready = sem("xb_ready")
        xp_ready = sem("xp_ready")
        xt_ready = sem("xt_ready")
        mp_ready = sem("mp_ready")
        mp_out = sem("mp_out")
        a_hi = sem("a_hi")
        a_lo = sem("a_lo")
        probs_ready = sem("probs_ready")
        out_done = sem("out_done")

        table = emb.rearrange("c v e -> (c v) e")

        def stage_view(n):
            return stage[n % STAGES]

        def w_hi_of(n):
            return w2h[:, n, :] if n < M1 else w3h[:, 2 * (n - M1):2 * (n - M1) + 2, :].rearrange("p k n -> p (k n)")

        def w_lo_of(n):
            return w2l[:, n, :] if n < M1 else w3l[:, 2 * (n - M1):2 * (n - M1) + 2, :].rearrange("p k n -> p (k n)")

        def bias(name, m):
            return sm[:, COLS[name] + m:COLS[name] + m + 1]

        block = ctx.enter_context(nc.Block())

        @block.sync
        def _(sp):
            sp.dma_start(idx[:], cat_idx.rearrange("(t p) c -> p t c", p=P)).then_inc(idx_in, 16)
            sp.dma_start(xc[:], x_t).then_inc(bottom_in, 16)
            sp.dma_start(wd1_sb[:], wd1).then_inc(bottom_in, 16)
            sp.dma_start(sm[:], small).then_inc(small_in, 16)
            sp.dma_start(wd2_sb[:], wd2.rearrange("(k p) n -> p k n", p=P)).then_inc(wd2_in, 16)
            sp.dma_start(wdf_sb[:], wdf.rearrange("(k p) n -> p k n", p=P)).then_inc(wd2_in, 16)
            sp.dma_start(bo_sb[:], bo).then_inc(small_in, 16)

            def load_stage(n):
                at_least(sp, w_lo, n - STAGES + 1)
                if n < M1:
                    src, dst = wt2[n * P:(n + 1) * P, :], stage_view(n)
                else:
                    k = 2 * (n - M1)
                    src = wt3[k * P:(k + 2) * P, :].rearrange("(k p) n -> p k n", p=P)
                    dst = stage_view(n).rearrange("p (k n) -> p k n", k=2)
                sp.dma_start(dst, src).then_inc(stage_in[n % STAGES], 16)

            for n in range(4):
                load_stage(n)
            for c in range(PAIR_CHUNKS):
                sp.dma_start(w1[0:PC, c, :], wt1[c * PC:(c + 1) * PC, :]).then_inc(w1_in, 16)
            sp.dma_start(w1[:, 3, :], wt1[PAIRS:PAIRS + E, :]).then_inc(w1_in, 16)
            for n in range(4, SPLIT_LOADS):
                load_stage(n)
            sp.dma_start(w4[:], wt4.rearrange("(k p) n -> p k n", p=P)).then_inc(w4_in, 16)
            sp.wait_ge(probs_ready, 1)
            sp.dma_start(out.rearrange("b o -> o b"), logits[:]).then_inc(out_done, 16)
            sp.wait_ge(out_done, 16)

        @block.gpsimd
        def _(pool):
            pool.iota(base[:], pattern=[[0, TILES], [VOCAB, N_CAT]], base=0, channel_multiplier=0).then_inc(base_made, 1)
            pool.memset(ident[:], 0.0).then_inc(ident_made, 1)
            pool.wait_ge(ident_made, 1)
            pool.affine_select(out=ident[:], in_=ident[:], compare_op=ALU.not_equal, fill=1.0, base=0,
                               pattern=[[-1, P]], channel_multiplier=1).then_inc(ident_made, 1)
            pool.wait_ge(idx_step, 4)
            for t in range(TILES):
                if t == 1:
                    pool.wait_ge(w_lo, SPLIT_LOADS)
                at_least(pool, tp_ready, (NG + 1) * (t - 2) + NG)
                for g, (f0, nf) in enumerate(Z_GROUPS):
                    for f in range(f0, f0 + nf):
                        pool.indirect_dma_start(
                            out=rows[t % 2][:, f, :], out_offset=None, in_=table,
                            in_offset=bass.IndirectOffsetOnAxis(ap=row_of[:, t, f:f + 1].bitcast(U32), axis=0),
                        ).then_inc(gathered[t % 2][g], 16)

        @block.tensor
        def _(pe):
            pe.wait_ge(bottom_in, 32)
            n = 0
            for m in range(4):
                at_least(pe, bot_out, n - 1)
                pe.matmul(mp[:, n % 2, :], wd1_sb[:, m * P:(m + 1) * P], xc[:], start=True, stop=True).then_inc(bot_ready, 1)
                n += 1
            pe.wait_ge(wd2_in, 32)
            for m in range(2):
                at_least(pe, bot_out, n - 1)
                for k in range(4):
                    if m == 0:
                        pe.wait_ge(bot_out, k + 1)
                    last = pe.matmul(mp[:, n % 2, :], wd2_sb[:, k, m * P:(m + 1) * P], h1[:, k, :], start=(k == 0), stop=(k == 3))
                last.then_inc(bot_ready, 1)
                n += 1
            for k in range(2):
                pe.wait_ge(bot_out, 4 + k + 1)
                last = pe.matmul(mp[:, n % 2, :], wdf_sb[:, k, :], h2[:, k, :], start=(k == 0), stop=(k == 1))
            last.then_inc(bot_ready, 1)

            pe.wait_ge(ident_made, 2)

            def transpose_features(t):
                for g, (f0, nf) in enumerate(Z_GROUPS):
                    pe.wait_ge(gathered[t % 2][g], 16 * nf * (t // 2 + 1))
                    if g == 1:
                        at_least(pe, xt_ready, t)
                    elif g % 2 == 0:
                        at_least(pe, zt_act, 4 * t + g // 2)
                    else:
                        at_least(pe, zt_dve, 4 * t + 1 + g // 2)
                    for f in range(nf):
                        last = pe.transpose(tp[:, g % 2, f * P:(f + 1) * P], rows[t % 2][:, f0 + f, :], ident[:])
                    last.then_inc(tp_ready, 1)

            def gram(t):
                pe.wait_ge(zt_act, 4 * t + 4)
                pe.wait_ge(zt_dve, 4 * t + 4)
                for r in range(ROUNDS):
                    at_least(pe, ex_act, ROUNDS * t + r - 1)
                    at_least(pe, ex_dve, ROUNDS * t + r - 1)
                    for k in range(ROUND):
                        g = ROUND * r + k
                        bank = 2 * (r % 2) + k // 4
                        last = pe.matmul(gp[:, bank, Q * NZ * (k % 4):Q * NZ * (k % 4 + 1)],
                                         zt[:, g, :, :].rearrange("p q f -> p (q f)"), zt[:, g, :, 0:NZ], start=True, stop=True)
                    last.then_inc(gram_ready, 1)

            def transpose_pairs(t):
                pe.wait_ge(xp_ready, t + 1)
                pe.wait_ge(zt_dve, 4 * t + 4)
                for c in range(PAIR_CHUNKS):
                    src = xp[:, IC * c:IC * (c + 1), :].rearrange("p i d -> p (i d)")
                    last = pe.transpose(tp[0:PC, 1, c * P:(c + 1) * P], src, ident[:])
                last.then_inc(tp_ready, 1)

            def chunk(t, c):
                at_least(pe, mp_out, CH * t + max(c - 1, 0))
                return mp[:, c % 2, 0:P]

            def layers(t):
                c = 0
                for m in range(M1):
                    o = chunk(t, c)
                    cols = slice(m * P, (m + 1) * P)
                    if t == 0 and m == 0:
                        pe.wait_ge(w1_in, 64)
                    pe.matmul(o, w1[:, 3, cols], dense_t[:, t * P:(t + 1) * P], start=True, stop=False)
                    if m == 0:
                        pe.wait_ge(xt_ready, t + 1)
                    for k in range(PAIR_CHUNKS):
                        last = pe.matmul(o, w1[0:PC, k, cols], xt[0:PC, k, :], start=False, stop=(k == 2))
                    last.then_inc(mp_ready, 1)
                    c += 1
                for wh, wl, ah, al, nk, nm, first in ((w2h, w2l, a1h, a1l, M1, M2, 0), (w3h, w3l, a2h, a2l, M2, M3, M1 // 2)):
                    if t == 0:
                        pe.wait_ge(w_lo, M1 if first == 0 else SPLIT_LOADS)
                    for m in range(nm):
                        o = chunk(t, c)
                        cols = slice(m * P, (m + 1) * P)
                        for k in range(nk):
                            if m == 0 and k % 2 == 0:
                                pe.wait_ge(a_lo, 8 * t + first + k // 2 + 1)
                            pe.matmul(o, wl[:, k, cols], ah[:, k, :], start=(k == 0), stop=False)
                            pe.matmul(o, wh[:, k, cols], al[:, k, :], start=False, stop=False)
                            last = pe.matmul(o, wh[:, k, cols], ah[:, k, :], start=False, stop=(k == nk - 1))
                        last.then_inc(mp_ready, 1)
                        c += 1
                if t == 0:
                    pe.wait_ge(w4_in, 16)
                for m in range(M4):
                    o = chunk(t, c)
                    for k in range(M3):
                        if m == 0:
                            pe.wait_ge(mp_out, CH * t + M1 + M2 + k + 1)
                        last = pe.matmul(o, w4[:, k, m * P:(m + 1) * P], a3[:, k, :], start=(k == 0), stop=(k == M3 - 1))
                    last.then_inc(mp_ready, 1)
                    c += 1
                o = chunk(t, c)
                for k in range(M4):
                    pe.wait_ge(mp_out, CH * t + M1 + M2 + M3 + k + 1)
                    last = pe.matmul(o[0:1, :], bias("Wo", k), a4[:, k, :], start=(k == 0), stop=(k == M4 - 1))
                last.then_inc(mp_ready, 1)

            for t in range(TILES):
                transpose_features(t)
                gram(t)
                transpose_pairs(t)
                layers(t)

        def extract(copy, r, q):
            b = 2 * (r % 2)
            src = gp[32 * q:32 * q + 32, b:b + 2, 0:4 * Q * NZ].rearrange("p k (g c) -> p k g c", g=4)[:, :, :, NZ * q:NZ * (q + 1)]
            dst = s_ij[32 * q:32 * q + 32, :, ROUND * r:ROUND * (r + 1)].rearrange("p j (k g) -> p k g j", k=2)
            return copy(dst, src)

        def evacuate_features(copy, g):
            f0, nf = Z_GROUPS[g]
            return copy(zt[:, :, :, f0:f0 + nf].rearrange("p g q f -> p f q g"),
                        tp[:, g % 2, 0:nf * P].rearrange("p (f q g) -> p f q g", f=nf, q=Q))

        @block.scalar
        def _(sc):
            def split_hi(n):
                sc.wait_ge(stage_in[n % STAGES], 16 * (n // STAGES + 1))
                sc.copy(w_hi_of(n), stage_view(n)).then_inc(w_hi, 1)

            sc.wait_ge(small_in, 32)
            n_split = 0
            for n in range(7):
                name, dst = (("bd1", h1[:, n, :]) if n < 4 else ("bd2", h2[:, n - 4, :]) if n < 6 else ("bdf", dense_t[:]))
                sc.wait_ge(bot_ready, n + 1)
                sc.activation(dst, mp[:, n % 2, :], ACT.Relu, bias=bias(name, n if n < 4 else n - 4 if n < 6 else 0)).then_inc(bot_out, 1)
                if n >= 2:
                    split_hi(n_split)
                    n_split += 1

            sc.wait_ge(zt_zeroed, 1)
            for t in range(TILES):
                for g in range(0, NG, 2):
                    sc.wait_ge(tp_ready, (NG + 1) * t + g + 1)
                    evacuate_features(sc.copy, g).then_inc(zt_act, 1)
                    for _i in range(2):
                        if t == 0 and n_split < SPLIT_LOADS:
                            split_hi(n_split)
                            n_split += 1
                at_least(sc, xb_ready, 2 * t)
                for r in range(ROUNDS):
                    sc.wait_ge(gram_ready, ROUNDS * t + r + 1)
                    extract(sc.copy, r, 0)
                    extract(sc.copy, r, 1).then_inc(ex_act, 1)
                c = 0
                for name, nm in (("bt1", M1), ("bt2", M2), ("bt3", M3), ("bt4", M4)):
                    for m in range(nm):
                        sc.wait_ge(mp_ready, CH * t + c + 1)
                        if name in ("bt1", "bt2"):
                            at_least(sc, a_lo, 8 * t + (c // 2) - 1)
                            dst = act[:, c % 4, :]
                        else:
                            dst = (a3 if name == "bt3" else a4)[:, m, :]
                        sc.activation(dst, mp[:, c % 2, 0:P], ACT.Relu,
                                      bias=bias(name, m)).then_inc(mp_out, 1)
                        c += 1
                sc.wait_ge(mp_ready, CH * t + c + 1)
                sc.activation(logits[:, t * P:(t + 1) * P], mp[0:1, c % 2, 0:P],
                              ACT.Identity, bias=bo_sb[:]).then_inc(mp_out, 1)
            sc.wait_ge(mp_out, CH * TILES)
            sc.activation(logits[:], logits[:], ACT.Sigmoid).then_inc(probs_ready, 1)

        @block.vector
        def _(ve):
            ve.wait_ge(idx_in, 16)
            ve.tensor_scalar(idx_clip[:], idx[:], float(-VOCAB), float(VOCAB - 1), ALU.max, ALU.min).then_inc(idx_step, 1)
            ve.wait_ge(idx_step, 1)
            ve.tensor_scalar(idx_neg[:], idx_clip[:], 0.0, float(VOCAB), ALU.is_lt, ALU.mult).then_inc(idx_step, 1)
            ve.wait_ge(idx_step, 2)
            ve.tensor_tensor(idx_wrap[:], idx_clip[:], idx_neg[:], ALU.add).then_inc(idx_step, 1)
            ve.wait_ge(idx_step, 3)
            ve.wait_ge(base_made, 1)
            ve.tensor_tensor(row_of[:], idx_wrap[:], base[:], ALU.add).then_inc(idx_step, 1)
            ve.memset(zt[:, :, :, NZ:32], 0.0).then_inc(zt_zeroed, 1)

            def split_lo(n):
                ve.wait_ge(w_hi, n + 1)
                ve.tensor_tensor(w_lo_of(n), stage_view(n), w_hi_of(n).bitcast(F32), ALU.subtract).then_inc(w_lo, 1)

            n_split = 0
            while n_split < 5:
                split_lo(n_split)
                n_split += 1
            ve.wait_ge(bot_out, 7)
            for t in range(TILES):
                at_least(ve, gram_ready, ROUNDS * t)
                ve.tensor_copy(zt[:, :, :, N_CAT].rearrange("p g q -> p q g"),
                               dense_t[:, t * P:(t + 1) * P].rearrange("p (q g) -> p q g", q=Q)).then_inc(zt_dve, 1)
                for g in range(1, NG, 2):
                    ve.wait_ge(tp_ready, (NG + 1) * t + g + 1)
                    evacuate_features(ve.tensor_copy, g).then_inc(zt_dve, 1)
                    for _i in range(3):
                        if t == 0 and n_split < SPLIT_LOADS:
                            split_lo(n_split)
                            n_split += 1
                for r in range(ROUNDS):
                    ve.wait_ge(gram_ready, ROUNDS * t + r + 1)
                    extract(ve.tensor_copy, r, 2)
                    extract(ve.tensor_copy, r, 3).then_inc(ex_dve, 1)
                ve.wait_ge(ex_act, ROUNDS * (t + 1))
                ve.wait_ge(ex_dve, ROUNDS * (t + 1))
                ve.transpose(xb[:, 0:NZ, :].rearrange("p j i -> p (j i)"), s_ij[:].rearrange("p j g -> p (j g)")).then_inc(xb_ready, 1)
                ve.transpose(xb[:, NZ:NZ + HALF, :].rearrange("p j i -> p (j i)"), s_ij[:, 0:HALF, :].rearrange("p j g -> p (j g)")).then_inc(xb_ready, 1)
                ve.wait_ge(xb_ready, 2 * (t + 1))
                flat = xb[:].rearrange("p j i -> p (j i)")
                diagonals = bass.AP(tensor=flat.tensor, offset=flat.offset + 32, ap=[list(flat.ap[0]), [33, NZ], [32, HALF]])
                ve.tensor_copy(xp[:], diagonals).then_inc(xp_ready, 1)
                ve.wait_ge(tp_ready, (NG + 1) * (t + 1))
                ve.tensor_copy(xt[0:PC, :, :], tp[0:PC, 1, 0:PAIR_CHUNKS * P].rearrange("p (c b) -> p c b", c=PAIR_CHUNKS)).then_inc(xt_ready, 1)
                for n in range((M1 + M2) // 2):
                    ah, al = (a1h, a1l) if n < M1 // 2 else (a2h, a2l)
                    k = 2 * n if n < M1 // 2 else 2 * n - M1
                    src = act[:, 2 * (n % 2):2 * (n % 2) + 2, :]
                    ve.wait_ge(mp_out, CH * t + 2 * n + 2)
                    ve.tensor_copy(ah[:, k:k + 2, :], src).then_inc(a_hi, 1)
                    ve.wait_ge(a_hi, 8 * t + n + 1)
                    ve.tensor_tensor(al[:, k:k + 2, :], src, ah[:, k:k + 2, :].bitcast(F32), ALU.subtract).then_inc(a_lo, 1)


def pair_rows():
    rows = []
    for i in range(NZ):
        for d in range(1, HALF + 1):
            lo, hi = sorted((i, (i + d) % NZ))
            rows.append(lo * (2 * NZ - lo - 1) // 2 + hi - lo - 1)
    return rows


def kernel(**inputs):
    import numpy as np
    import concourse.bacc as bacc
    from concourse.bass_utils import run_bass_kernel_spmd as run

    a = {k.replace("L0_rec_", ""): np.asarray(v) for k, v in inputs.items()}
    small = np.concatenate([a[n].reshape(-1, P).T for n in COLS], axis=1)
    order = pair_rows() + list(range(PAIRS, PAIRS + E))
    laid_out = {
        "x_t": a["r_dense_x"].T, "cat_idx": a["r_cat_idx"], "emb": a["emb_table"], "small": small,
        "bo": a["bo"].reshape(1, 1), "wd1": a["Wd1"], "wd2": a["Wd2"], "wdf": a["Wdf"],
        "wt1": a["Wt1"][order], "wt2": a["Wt2"], "wt3": a["Wt3"], "wt4": a["Wt4"],
    }
    nc = bacc.Bacc("TRN2", target_bir_lowering=False, num_devices=1)
    arrays, args = {}, []
    for name, x in laid_out.items():
        x = np.ascontiguousarray(x)
        arrays[f"in_{name}"] = x
        args.append(nc.dram_tensor(f"in_{name}", x.shape, mybir.dt.from_np(x.dtype), kind="ExternalInput").ap())
    args.append(nc.dram_tensor("out_0", (BATCH, 1), F32, kind="ExternalOutput").ap())
    build(nc, *args)
    r = run(nc, [arrays], core_ids=[0])
    return r.results[0]["out_0"]
```

```python
import concourse.bass as bass
from concourse import mybir
from contextlib import ExitStack

F32 = mybir.dt.float32
F32R = mybir.dt.float32r
I32 = mybir.dt.int32
U32 = mybir.dt.uint32
ALU = mybir.AluOpType
ACT = mybir.ActivationFunctionType

P = 128
N_CAT, N_CONT, E, VOCAB = 26, 13, 128, 12500
BATCH = 512
TILES = BATCH // P
NZ = N_CAT + 1
HALF = NZ // 2
PAIRS = NZ * HALF
PAIR_CHUNKS = 3
IC = NZ // PAIR_CHUNKS
PC = IC * HALF
Q = 4
GROUPS = P // Q
GRAM_M = 32 * (Q - 1) + NZ
ROUND = 8
ROUNDS = GROUPS // ROUND
ZG = 4
Z_GROUPS = [(f, min(ZG, N_CAT - f)) for f in range(0, N_CAT, ZG)]
NG = len(Z_GROUPS)
BOT = [N_CONT, 512, 256, E]
TOP = [PAIRS + E, 1024, 1024, 512, 256]
M1, M2, M3 = (n // P for n in TOP[1:4])
HALF2 = TOP[2] // 2
FEATURE_SLOTS = 42
STAGES = 4
SPLIT_LOADS = M1 + M2 // 2

COLS = {}
_at = 0
for _name, _n in (("bd1", 4), ("bd2", 2), ("bdf", 1), ("bt1", M1), ("bt2", M2), ("bt3", M3), ("bo", 1)):
    COLS[_name] = _at
    _at += _n
N_SMALL = _at


def at_least(engine, sem, n):
    if n > 0:
        engine.wait_ge(sem, n)


def build(nc, x_t, cat_idx, emb, small, rows4, wd1, wd2, wdf, wt1, wt2, wt3, wt4, out):
    ctx = ExitStack()
    with ctx:
        def sb(name, shape, dt=F32, where=ctx):
            return where.enter_context(nc.sbuf_tensor(name, shape, dt))

        def pb(name, shape, dt=F32):
            return ctx.enter_context(nc.psum_tensor(name, shape, dt))

        def sem(name):
            return ctx.enter_context(nc.semaphore(name))

        w1 = sb("w1", [P, 4, TOP[1]])
        w2h = sb("w2h", [P, M1, TOP[2]], F32R)
        w2l = sb("w2l", [P, M1, TOP[2]], F32R)
        w3h = sb("w3h", [P, M2, TOP[3]], F32R)
        w3l = sb("w3l", [P, M2, TOP[3]], F32R)
        w4 = sb("w4", [P, M3, TOP[4]])
        sm = sb("sm", [P, N_SMALL])
        b4_wo = sb("b4_wo", [P, 2, TOP[4]])
        rows = [sb(f"rows{h}", [P, N_CAT, E]) for h in range(2)]
        zt = sb("zt", [P, GROUPS, Q, 32])
        s_ij = sb("s_ij", [P, NZ, GROUPS])
        xb = sb("xb", [P, NZ + HALF, 32])
        xp = sb("xp", [P, NZ, HALF])
        xt = sb("xt", [P, PAIR_CHUNKS, P])
        dense_t = sb("dense_t", [P, BATCH])
        ident = sb("ident", [P, P])
        idx = sb("idx", [P, TILES, N_CAT], I32)
        idx_neg = sb("idx_neg", [P, TILES, N_CAT], I32)
        idx_clip = sb("idx_clip", [P, TILES, N_CAT], I32)
        idx_wrap = sb("idx_wrap", [P, TILES, N_CAT], I32)
        row_of = sb("row_of", [P, TILES, N_CAT], I32)
        base = sb("base", [P, TILES, N_CAT], I32)
        act = sb("act", [P, 4, P])
        a3 = sb("a3", [P, M3, P])
        z4 = sb("z4", [P, 2, TOP[4]])
        logits = sb("logits", [P, TILES])
        probs = sb("probs", [P, TILES])

        with ExitStack() as early:
            xc = sb("xc", [N_CONT, BATCH], where=early)
            wd1_sb = sb("wd1_sb", [N_CONT, BOT[1]], where=early)
            wd2_sb = sb("wd2_sb", [P, 4, BOT[2]], where=early)
            wdf_sb = sb("wdf_sb", [P, 2, BOT[3]], where=early)
            h1 = sb("h1", [P, 4, BATCH], where=early)
            h2 = sb("h2", [P, 2, BATCH], where=early)
            stage01 = sb("stage01", [P, 1, 1024], where=early)
        a1h = sb("a1h", [P, M1, P], F32R)
        a1l = sb("a1l", [P, M1, P], F32R)
        a2h = sb("a2h", [P, M2, P], F32R)
        a2l = sb("a2l", [P, M2, P], F32R)
        raw = sb("raw", [P, 2, HALF2])
        stage = [rows[1][:, 8 * i:8 * i + 8, :].rearrange("p f e -> p (f e)") for i in range(3)]
        stage += [stage01[:, i, :] for i in range(1)]

        tp = pb("tp", [P, 2, 512])
        gp = pb("gp", [P, 4, 512])
        mp = pb("mp", [P, 2, 512])

        idx_in = sem("idx_in")
        small_in = sem("small_in")
        bottom_in = sem("bottom_in")
        wd2_in = sem("wd2_in")
        w1_in = sem("w1_in")
        w4_in = sem("w4_in")
        stage_in = [sem(f"stage_in{i}") for i in range(STAGES)]
        base_made = sem("base_made")
        ident_made = sem("ident_made")
        zt_zeroed = sem("zt_zeroed")
        idx_step = sem("idx_step")
        gathered = [[sem(f"gathered{h}_{g}") for g in range(NG)] for h in range(2)]
        bot_ready = sem("bot_ready")
        bot_out = sem("bot_out")
        w_hi = sem("w_hi")
        w_lo = sem("w_lo")
        ft_ready = sem("ft_ready")
        zt_act = sem("zt_act")
        zt_dve = sem("zt_dve")
        gram_ready = sem("gram_ready")
        ex_act = sem("ex_act")
        ex_dve = sem("ex_dve")
        xb_ready = sem("xb_ready")
        xp_ready = sem("xp_ready")
        pairs_ready = sem("pairs_ready")
        xt_ready = sem("xt_ready")
        l1_ready = sem("l1_ready")
        l1_out = sem("l1_out")
        a_hi = sem("a_hi")
        a_lo = sem("a_lo")
        l2_ready = sem("l2_ready")
        l3_ready = sem("l3_ready")
        raw_ready = sem("raw_ready")
        turned = sem("turned")
        relu_act = sem("relu_act")
        relu_dve = sem("relu_dve")
        a3_ready = sem("a3_ready")
        l4_ready = sem("l4_ready")
        z4_ready = sem("z4_ready")
        logits_ready = sem("logits_ready")
        probs_ready = sem("probs_ready")
        out_done = sem("out_done")

        table = emb.rearrange("c v e -> (c v) e")

        def stage_view(n):
            return stage[n % STAGES]

        def w_hi_of(n):
            return w2h[:, n, :] if n < M1 else w3h[:, 2 * (n - M1):2 * (n - M1) + 2, :].rearrange("p k n -> p (k n)")

        def w_lo_of(n):
            return w2l[:, n, :] if n < M1 else w3l[:, 2 * (n - M1):2 * (n - M1) + 2, :].rearrange("p k n -> p (k n)")

        def bias(name, m):
            return sm[:, COLS[name] + m:COLS[name] + m + 1]

        def l1_bank(m):
            return mp[:, m % 6, 0:P] if m % 6 < 2 else gp[:, m % 6 - 2, 0:P]

        def extract(copy, r, q):
            b = 2 * (r % 2)
            src = gp[32 * q:32 * q + NZ, b:b + 2, 0:4 * Q * NZ].rearrange("p k (g c) -> p k g c", g=4)[:, :, :, NZ * q:NZ * (q + 1)]
            dst = s_ij[32 * q:32 * q + NZ, :, ROUND * r:ROUND * (r + 1)].rearrange("p j (k g) -> p k g j", k=2)
            return copy(dst, src)

        def evacuate_features(copy, g):
            f0, nf = Z_GROUPS[g]
            return copy(zt[:, :, :, f0:f0 + nf].rearrange("p g q f -> p f q g"),
                        gp[:, g % 4, 0:nf * P].rearrange("p (f q g) -> p f q g", f=nf, q=Q))

        block = ctx.enter_context(nc.Block())

        @block.sync
        def _(sp):
            sp.dma_start(idx[:], cat_idx.rearrange("(t p) c -> p t c", p=P)).then_inc(idx_in, 16)
            sp.dma_start(xc[:], x_t).then_inc(bottom_in, 16)
            sp.dma_start(wd1_sb[:], wd1).then_inc(bottom_in, 16)
            sp.dma_start(sm[:], small).then_inc(small_in, 16)
            sp.dma_start(wd2_sb[:], wd2.rearrange("(k p) n -> p k n", p=P)).then_inc(wd2_in, 16)
            sp.dma_start(wdf_sb[:], wdf.rearrange("(k p) n -> p k n", p=P)).then_inc(wd2_in, 16)
            sp.dma_start(b4_wo[:].rearrange("p a n -> p (a n)"),
                         bass.AP(tensor=rows4.tensor, offset=rows4.offset, ap=[[0, P], [1, 2 * TOP[4]]])).then_inc(small_in, 16)

            def load_stage(n):
                at_least(sp, w_lo, n - STAGES + 1)
                if n < M1:
                    src, dst = wt2[n * P:(n + 1) * P, :], stage_view(n)
                else:
                    k = 2 * (n - M1)
                    src = wt3[k * P:(k + 2) * P, :].rearrange("(k p) n -> p k n", p=P)
                    dst = stage_view(n).rearrange("p (k n) -> p k n", k=2)
                sp.dma_start(dst, src).then_inc(stage_in[n % STAGES], 16)

            for n in range(SPLIT_LOADS):
                load_stage(n)
            for c in range(PAIR_CHUNKS):
                sp.dma_start(w1[0:PC, c, :], wt1[c * PC:(c + 1) * PC, :]).then_inc(w1_in, 16)
            sp.dma_start(w1[:, 3, :], wt1[PAIRS:PAIRS + E, :]).then_inc(w1_in, 16)
            sp.dma_start(w4[:], wt4.rearrange("(k p) n -> p k n", p=P)).then_inc(w4_in, 16)
            for t in range(TILES):
                sp.wait_ge(probs_ready, t + 1)
                sp.dma_start(out[t * P:(t + 1) * P, :], probs[:, t:t + 1]).then_inc(out_done, 16)
            sp.wait_ge(out_done, 16 * TILES)

        @block.gpsimd
        def _(pool):
            pool.iota(base[:], pattern=[[0, TILES], [VOCAB, N_CAT]], base=0, channel_multiplier=0).then_inc(base_made, 1)
            pool.memset(ident[:], 0.0).then_inc(ident_made, 1)
            pool.wait_ge(ident_made, 1)
            pool.affine_select(out=ident[:], in_=ident[:], compare_op=ALU.not_equal, fill=1.0, base=0,
                               pattern=[[-1, P]], channel_multiplier=1).then_inc(ident_made, 1)
            pool.wait_ge(idx_step, 4)
            for t in range(TILES):
                if t == 1:
                    pool.wait_ge(w_lo, SPLIT_LOADS)
                at_least(pool, ft_ready, NG * (t - 1))
                for g, (f0, nf) in enumerate(Z_GROUPS):
                    for f in range(f0, f0 + nf):
                        pool.indirect_dma_start(
                            out=rows[t % 2][:, f, :], out_offset=None, in_=table,
                            in_offset=bass.IndirectOffsetOnAxis(ap=row_of[:, t, f:f + 1].bitcast(U32), axis=0),
                        ).then_inc(gathered[t % 2][g], 16)

        @block.tensor
        def _(pe):
            pe.wait_ge(bottom_in, 32)
            n = 0
            for m in range(4):
                at_least(pe, bot_out, n - 1)
                pe.matmul(mp[:, n % 2, :], wd1_sb[:, m * P:(m + 1) * P], xc[:], start=True, stop=True).then_inc(bot_ready, 1)
                n += 1
            pe.wait_ge(wd2_in, 32)
            for m in range(2):
                at_least(pe, bot_out, n - 1)
                for k in range(4):
                    if m == 0:
                        pe.wait_ge(bot_out, k + 1)
                    last = pe.matmul(mp[:, n % 2, :], wd2_sb[:, k, m * P:(m + 1) * P], h1[:, k, :], start=(k == 0), stop=(k == 3))
                last.then_inc(bot_ready, 1)
                n += 1
            for k in range(2):
                pe.wait_ge(bot_out, 4 + k + 1)
                last = pe.matmul(mp[:, n % 2, :], wdf_sb[:, k, :], h2[:, k, :], start=(k == 0), stop=(k == 1))
            last.then_inc(bot_ready, 1)

            pe.wait_ge(ident_made, 2)

            def transpose_feature(t, f):
                g, n = f // ZG, f % ZG
                if n == 0:
                    pe.wait_ge(gathered[t % 2][g], 16 * Z_GROUPS[g][1] * (t // 2 + 1))
                    if g >= 4 and g % 2 == 0:
                        pe.wait_ge(zt_act, 4 * t + g // 2 - 1)
                    elif g >= 4:
                        pe.wait_ge(zt_dve, 4 * t + g // 2)
                turned_feature = pe.transpose(gp[:, g % 4, n * P:(n + 1) * P], rows[t % 2][:, f, :], ident[:])
                if n == Z_GROUPS[g][1] - 1:
                    turned_feature.then_inc(ft_ready, 1)

            def gram(t):
                pe.wait_ge(zt_act, 4 * t + 4)
                pe.wait_ge(zt_dve, 4 * t + 4)
                for r in range(ROUNDS):
                    if r >= 2:
                        pe.wait_ge(ex_act, ROUNDS * t + r - 1)
                        pe.wait_ge(ex_dve, ROUNDS * t + r - 1)
                    for k in range(ROUND):
                        g = ROUND * r + k
                        bank = 2 * (r % 2) + k // 4
                        last = pe.matmul(gp[0:GRAM_M, bank, Q * NZ * (k % 4):Q * NZ * (k % 4 + 1)],
                                         zt[:, g, :, :].rearrange("p q f -> p (q f)")[:, 0:GRAM_M], zt[:, g, :, 0:NZ], start=True, stop=True)
                    last.then_inc(gram_ready, 1)

            def transpose_pairs(t):
                pe.wait_ge(xp_ready, t + 1)
                for c in range(PAIR_CHUNKS):
                    src = xp[:, IC * c:IC * (c + 1), :].rearrange("p i d -> p (i d)")
                    last = pe.transpose(tp[0:PC, 0, c * P:(c + 1) * P], src, ident[:])
                last.then_inc(pairs_ready, 1)

            def layer_1_dense(t, m):
                if m in (2, 4):
                    pe.wait_ge(ex_act, ROUNDS * t + 2 + m // 2)
                    pe.wait_ge(ex_dve, ROUNDS * t + 2 + m // 2)
                if m >= 6:
                    pe.wait_ge(l1_out, M1 * t + m - 5)
                pe.matmul(l1_bank(m), w1[:, 3, m * P:(m + 1) * P], dense_t[:, t * P:(t + 1) * P], start=True, stop=False)

            def layer_1(t):
                for m in range(M1):
                    if m >= 6:
                        layer_1_dense(t, m)
                    for k in range(PAIR_CHUNKS):
                        last = pe.matmul(l1_bank(m), w1[0:PC, k, m * P:(m + 1) * P], xt[0:PC, k, :], start=False, stop=(k == PAIR_CHUNKS - 1))
                    last.then_inc(l1_ready, 1)

            def product(o, ah, al, wh, wl, k, n, cols, between):
                pe.matmul(o, al[:, k, :], wh[:, k, cols], start=(k == 0), stop=False)
                between()
                pe.matmul(o, ah[:, k, :], wl[:, k, cols], start=False, stop=False)
                between()
                last = pe.matmul(o, ah[:, k, :], wh[:, k, cols], start=False, stop=(k == n - 1))
                if k < n - 1:
                    between()
                return last

            def turn(t, h):
                pe.wait_ge(raw_ready, 3 * t + h + 1)
                if h == 0:
                    at_least(pe, z4_ready, t)
                if h == 1:
                    pe.wait_ge(relu_act, 4 * t + 2)
                    pe.wait_ge(relu_dve, 4 * t + 2)
                if h == 2:
                    pe.wait_ge(relu_act, 4 * t + 4)
                for c in range(4):
                    o = tp[:, c // 2, (c % 2) * P:(c % 2 + 1) * P] if h < 2 else tp[:, 0, c * P:(c + 1) * P]
                    last = pe.transpose(o, raw[:, h % 2, c * P:(c + 1) * P], ident[:])
                last.then_inc(turned, 1)

            def layers_2_3(t):
                slots = [0]

                def nothing():
                    pass

                def next_feature():
                    slots[0] += 1
                    f = slots[0] * N_CAT // FEATURE_SLOTS
                    if t + 1 < TILES and f <= N_CAT and f > (slots[0] - 1) * N_CAT // FEATURE_SLOTS:
                        transpose_feature(t + 1, f - 1)

                if t == 0:
                    pe.wait_ge(w_lo, M1)
                for h in range(2):
                    pe.wait_ge(l1_out, M1 * t + 7 + h)
                    for k in range(M1):
                        if h == 0 and k % 2 == 0:
                            pe.wait_ge(a_lo, 8 * t + k // 2 + 1)
                        if h == 1 and k == 4:
                            turn(t, 0)
                        last = product(mp[:, h, :], a1h, a1l, w2h, w2l, k, M1, slice(h * HALF2, (h + 1) * HALF2),
                                       next_feature if h else nothing)
                    last.then_inc(l2_ready, 1)
                if t == 0:
                    pe.wait_ge(w_lo, SPLIT_LOADS)
                for k in range(M2):
                    if k == 2:
                        turn(t, 1)
                    if k % 2 == 0:
                        pe.wait_ge(a_lo, 8 * t + 4 + k // 2 + 1)
                    last = product(mp[:, 0, :], a2h, a2l, w3h, w3l, k, M2, slice(0, TOP[3]), next_feature)
                last.then_inc(l3_ready, 1)

            def layer_4(t):
                if t == 0:
                    pe.wait_ge(w4_in, 16)
                for k in range(M3):
                    pe.wait_ge(a3_ready, M3 * t + k + 1)
                    last = pe.matmul(tp[:, 1, 0:TOP[4]], a3[:, k, :], w4[:, k, :], start=(k == 0), stop=(k == M3 - 1))
                last.then_inc(l4_ready, 1)

            for f in range(N_CAT):
                transpose_feature(0, f)
            gram(0)
            for t in range(TILES):
                if t == 0:
                    pe.wait_ge(w1_in, 64)
                for m in range(4):
                    layer_1_dense(t, m)
                transpose_pairs(t)
                for m in range(4, 6):
                    layer_1_dense(t, m)
                pe.wait_ge(xt_ready, t + 1)
                layer_1(t)
                layers_2_3(t)
                turn(t, 2)
                if t + 1 < TILES:
                    gram(t + 1)
                layer_4(t)

        @block.scalar
        def _(sc):
            def split_hi(n):
                sc.wait_ge(stage_in[n % STAGES], 16 * (n // STAGES + 1))
                sc.copy(w_hi_of(n), stage_view(n)).then_inc(w_hi, 1)

            sc.wait_ge(small_in, 32)
            n_split = 0
            for n in range(7):
                name, dst = (("bd1", h1[:, n, :]) if n < 4 else ("bd2", h2[:, n - 4, :]) if n < 6 else ("bdf", dense_t[:]))
                sc.wait_ge(bot_ready, n + 1)
                sc.activation(dst, mp[:, n % 2, :], ACT.Relu, bias=bias(name, n if n < 4 else n - 4 if n < 6 else 0)).then_inc(bot_out, 1)
                if n >= 2:
                    split_hi(n_split)
                    n_split += 1

            def features(t, g):
                sc.wait_ge(ft_ready, NG * t + g + 1)
                evacuate_features(sc.copy, g).then_inc(zt_act, 1)

            def gram(t):
                at_least(sc, xb_ready, 2 * t)
                for r in range(ROUNDS):
                    sc.wait_ge(gram_ready, ROUNDS * t + r + 1)
                    extract(sc.copy, r, 0)
                    extract(sc.copy, r, 1).then_inc(ex_act, 1)

            sc.wait_ge(zt_zeroed, 2)
            for g in range(0, NG, 2):
                features(0, g)
                if g == 0:
                    for n in range(n_split, SPLIT_LOADS):
                        split_hi(n)
            gram(0)
            for t in range(TILES):
                more = t + 1 < TILES
                for m in range(M1):
                    sc.wait_ge(l1_ready, M1 * t + m + 1)
                    at_least(sc, a_lo, 8 * t + m // 2 - 1)
                    sc.activation(act[:, m % 4, :], l1_bank(m), ACT.Relu, bias=bias("bt1", m)).then_inc(l1_out, 1)
                for h in range(2):
                    sc.wait_ge(l2_ready, 2 * t + h + 1)
                    sc.copy(raw[:, h, :], mp[:, h, :]).then_inc(raw_ready, 1)
                    if more and h == 0:
                        features(t + 1, 0)
                    sc.wait_ge(turned, 3 * t + h + 1)
                    sc.wait_ge(a_lo, 8 * t + 4 + 2 * h)
                    for c in range(2):
                        sc.activation(act[:, c, :], tp[:, 0, c * P:(c + 1) * P], ACT.Relu, bias=bias("bt2", 4 * h + c)).then_inc(relu_act, 1)
                    if more and h == 0:
                        features(t + 1, 2)
                if more:
                    features(t + 1, 4)
                    features(t + 1, 6)
                sc.wait_ge(l3_ready, t + 1)
                sc.copy(raw[:, 0, :], mp[:, 0, :]).then_inc(raw_ready, 1)
                sc.wait_ge(turned, 3 * t + 3)
                for c in range(M3):
                    sc.activation(a3[:, c, :], tp[:, 0, c * P:(c + 1) * P], ACT.Relu, bias=bias("bt3", c)).then_inc(a3_ready, 1)
                if more:
                    gram(t + 1)
                sc.wait_ge(logits_ready, t + 1)
                sc.activation(probs[:, t:t + 1], logits[:, t:t + 1], ACT.Sigmoid, bias=bias("bo", 0)).then_inc(probs_ready, 1)

        @block.vector
        def _(ve):
            ve.wait_ge(idx_in, 16)
            ve.tensor_scalar(idx_clip[:], idx[:], float(-VOCAB), float(VOCAB - 1), ALU.max, ALU.min).then_inc(idx_step, 1)
            ve.wait_ge(idx_step, 1)
            ve.tensor_scalar(idx_neg[:], idx_clip[:], 0.0, float(VOCAB), ALU.is_lt, ALU.mult).then_inc(idx_step, 1)
            ve.wait_ge(idx_step, 2)
            ve.tensor_tensor(idx_wrap[:], idx_clip[:], idx_neg[:], ALU.add).then_inc(idx_step, 1)
            ve.wait_ge(idx_step, 3)
            ve.wait_ge(base_made, 1)
            ve.tensor_tensor(row_of[:], idx_wrap[:], base[:], ALU.add).then_inc(idx_step, 1)
            ve.memset(s_ij[:], 0.0).then_inc(zt_zeroed, 1)
            ve.memset(zt[:, :, :, NZ:32], 0.0).then_inc(zt_zeroed, 1)

            def split_lo(n):
                ve.wait_ge(w_hi, n + 1)
                ve.tensor_tensor(w_lo_of(n), stage_view(n), w_hi_of(n).bitcast(F32), ALU.subtract).then_inc(w_lo, 1)

            for n in range(4):
                split_lo(n)
            ve.wait_ge(small_in, 32)
            ve.wait_ge(bot_out, 7)

            def last_layer(t):
                ve.wait_ge(l4_ready, t + 1)
                ve.tensor_tensor(z4[:, 0, :], tp[:, 1, 0:TOP[4]], b4_wo[:, 0, :], ALU.add).then_inc(z4_ready, 1)
                ve.wait_ge(z4_ready, t + 1)
                ve.scalar_tensor_tensor(out=z4[:, 1, :], in0=z4[:, 0, :], scalar=0.0, in1=b4_wo[:, 1, :], op0=ALU.max,
                                        op1=ALU.mult, accum_out=logits[:, t:t + 1]).then_inc(logits_ready, 1)

            def dense_feature(t):
                at_least(ve, gram_ready, ROUNDS * t)
                ve.tensor_copy(zt[:, :, :, N_CAT].rearrange("p g q -> p q g"),
                               dense_t[:, t * P:(t + 1) * P].rearrange("p (q g) -> p q g", q=Q)).then_inc(zt_dve, 1)

            def features(t, g):
                ve.wait_ge(ft_ready, NG * t + g + 1)
                evacuate_features(ve.tensor_copy, g).then_inc(zt_dve, 1)

            def gram(t):
                for r in range(ROUNDS):
                    ve.wait_ge(gram_ready, ROUNDS * t + r + 1)
                    extract(ve.tensor_copy, r, 2)
                    extract(ve.tensor_copy, r, 3).then_inc(ex_dve, 1)
                ve.wait_ge(ex_act, ROUNDS * (t + 1))
                ve.wait_ge(ex_dve, ROUNDS * (t + 1))
                ve.transpose(xb[:, 0:NZ, :].rearrange("p j i -> p (j i)"), s_ij[:].rearrange("p j g -> p (j g)")).then_inc(xb_ready, 1)
                ve.transpose(xb[:, NZ:NZ + HALF, :].rearrange("p j i -> p (j i)"), s_ij[:, 0:HALF, :].rearrange("p j g -> p (j g)")).then_inc(xb_ready, 1)
                ve.wait_ge(xb_ready, 2 * (t + 1))
                flat = xb[:].rearrange("p j i -> p (j i)")
                diagonals = bass.AP(tensor=flat.tensor, offset=flat.offset + 32, ap=[list(flat.ap[0]), [33, NZ], [32, HALF]])
                ve.tensor_copy(xp[:], diagonals).then_inc(xp_ready, 1)

            def split(t, n, ah, al, k, src):
                ve.tensor_copy(ah[:, k:k + 2, :], src).then_inc(a_hi, 1)
                ve.wait_ge(a_hi, 8 * t + n + 1)
                ve.tensor_tensor(al[:, k:k + 2, :], src, ah[:, k:k + 2, :].bitcast(F32), ALU.subtract).then_inc(a_lo, 1)

            dense_feature(0)
            features(0, 1)
            for n in range(4, SPLIT_LOADS):
                split_lo(n)
            features(0, 3)
            features(0, 5)
            gram(0)
            for t in range(TILES):
                more = t + 1 < TILES
                ve.wait_ge(pairs_ready, t + 1)
                ve.tensor_copy(xt[0:PC, :, :], tp[0:PC, 0, 0:PAIR_CHUNKS * P].rearrange("p (c b) -> p c b", c=PAIR_CHUNKS)).then_inc(xt_ready, 1)
                if t >= 1:
                    last_layer(t - 1)
                if more:
                    dense_feature(t + 1)
                for n in range(M1 // 2):
                    ve.wait_ge(l1_out, M1 * t + 2 * n + 2)
                    split(t, n, a1h, a1l, 2 * n, act[:, 2 * (n % 2):2 * (n % 2) + 2, :])
                for h in range(2):
                    ve.wait_ge(turned, 3 * t + h + 1)
                    ve.wait_ge(a_lo, 8 * t + 4 + 2 * h)
                    for c in range(2):
                        ve.tensor_scalar(act[:, 2 + c, :], tp[:, 1, c * P:(c + 1) * P], bias("bt2", 4 * h + 2 + c), 0.0,
                                         ALU.add, ALU.max).then_inc(relu_dve, 1)
                    ve.wait_ge(relu_act, 4 * t + 2 * h + 2)
                    split(t, 4 + 2 * h, a2h, a2l, 4 * h, act[:, 0:2, :])
                    ve.wait_ge(relu_dve, 4 * t + 2 * h + 2)
                    split(t, 5 + 2 * h, a2h, a2l, 4 * h + 2, act[:, 2:4, :])
                    if more and h == 0:
                        features(t + 1, 1)
                if more:
                    features(t + 1, 3)
                    features(t + 1, 5)
                    gram(t + 1)
            last_layer(TILES - 1)


def pair_rows():
    rows = []
    for i in range(NZ):
        for d in range(1, HALF + 1):
            lo, hi = sorted((i, (i + d) % NZ))
            rows.append(lo * (2 * NZ - lo - 1) // 2 + hi - lo - 1)
    return rows


def kernel(**inputs):
    import numpy as np
    import concourse.bacc as bacc
    from concourse.bass_utils import run_bass_kernel_spmd as run

    a = {k.replace("L0_rec_", ""): np.asarray(v) for k, v in inputs.items()}
    small = np.concatenate([np.broadcast_to(a[n], (P, 1)) if n == "bo" else a[n].reshape(-1, P).T for n in COLS], axis=1)
    order = pair_rows() + list(range(PAIRS, PAIRS + E))
    laid_out = {
        "x_t": a["r_dense_x"].T, "cat_idx": a["r_cat_idx"], "emb": a["emb_table"], "small": small,
        "rows4": np.concatenate([a["bt4"].reshape(1, -1), a["Wo"].reshape(1, -1)], axis=1), "wd1": a["Wd1"], "wd2": a["Wd2"], "wdf": a["Wdf"],
        "wt1": a["Wt1"][order], "wt2": a["Wt2"], "wt3": a["Wt3"], "wt4": a["Wt4"],
    }
    nc = bacc.Bacc("TRN2", target_bir_lowering=False, num_devices=1)
    arrays, args = {}, []
    for name, x in laid_out.items():
        x = np.ascontiguousarray(x)
        arrays[f"in_{name}"] = x
        args.append(nc.dram_tensor(f"in_{name}", x.shape, mybir.dt.from_np(x.dtype), kind="ExternalInput").ap())
    args.append(nc.dram_tensor("out_0", (BATCH, 1), F32, kind="ExternalOutput").ap())
    build(nc, *args)
    r = run(nc, [arrays], core_ids=[0])
    return r.results[0]["out_0"]
```

```python
import concourse.bass as bass
from concourse import mybir
from contextlib import ExitStack

F32 = mybir.dt.float32
F32R = mybir.dt.float32r
I32 = mybir.dt.int32
U32 = mybir.dt.uint32
ALU = mybir.AluOpType
ACT = mybir.ActivationFunctionType

P = 128
N_CAT, N_CONT, E, VOCAB = 26, 13, 128, 12500
BATCH = 512
TILES = BATCH // P
BOT = [N_CONT, 512, 256, E]

NZ = N_CAT + 1
HALF = NZ // 2
PAIRS = NZ * HALF
PAIR_CHUNKS = 3
IC = NZ // PAIR_CHUNKS
PC = IC * HALF
TOP = [PAIRS + E, 1024, 1024, 512, 256]
M1, M2, M3 = (n // P for n in TOP[1:4])
HALF2 = TOP[2] // 2

Q = 4
GROUPS = P // Q
NZE = NZ + NZ % 2
GRAM_M = 32 * (Q - 1) + NZE
ROUND = 4
ROUNDS = GROUPS // ROUND
ZG = 4
Z_GROUPS = [(f, min(ZG, N_CAT - f)) for f in range(0, N_CAT, ZG)]
NG = len(Z_GROUPS)
FEATURE_SLOTS = [(7, 32)] + [(1, 18)] * (TILES - 1)
GRAM_SLOTS = [(35, 59)] + [(23, 46)] * (TILES - 1)
RELU_ROUND = [1] + [4] * (TILES - 1)
SPLIT_LOADS = M1 + M2 // 2

COLS = {}
_at = 0
for _name, _n in (("bd1", 4), ("bd2", 2), ("bdf", 1), ("bt1", M1), ("bt2", M2), ("bt3", M3), ("bo", 1)):
    COLS[_name] = _at
    _at += _n
N_SMALL = _at


def at_least(engine, sem, n):
    if n > 0:
        engine.wait_ge(sem, n)


def build(nc, x_t, cat_idx, emb, small, rows4, wd1, wd2, wdf, wt1, wt2, wt3, wt4, out):
    ctx = ExitStack()
    with ctx:
        def sb(name, shape, dt=F32, where=ctx):
            return where.enter_context(nc.sbuf_tensor(name, shape, dt))

        def pb(name, shape, dt=F32):
            return ctx.enter_context(nc.psum_tensor(name, shape, dt))

        def sem(name):
            return ctx.enter_context(nc.semaphore(name))

        w1 = sb("w1", [P, PAIR_CHUNKS, TOP[1]])
        w2h = sb("w2h", [P, M1, TOP[2]], F32R)
        w3h = sb("w3h", [P, M2, TOP[3]], F32R)
        with ExitStack() as whole:
            w2 = sb("w2", [P, M1, TOP[2]], where=whole)
            w3 = sb("w3", [P, M2, TOP[3]], where=whole)
        w2l = sb("w2l", [P, M1, TOP[2]], F32R)
        w3l = sb("w3l", [P, M2, TOP[3]], F32R)
        w4 = sb("w4", [P, M3, TOP[4]])
        sm = sb("sm", [P, N_SMALL])
        b4_wo = sb("b4_wo", [P, 2, TOP[4]])
        rows = sb("rows", [P, N_CAT, E])
        zt = sb("zt", [P, GROUPS, 2, Q, 32], F32R)
        s_ij = sb("s_ij", [P, NZ, GROUPS])
        raw = sb("raw", [P, 2, HALF2])
        xt = sb("xt", [P, PAIR_CHUNKS, P])
        dense_t = sb("dense_t", [P, BATCH])
        pre = sb("pre", [P, M1, BATCH])
        ident = sb("ident", [P, P])
        row_of = sb("row_of", [P, TILES, N_CAT], I32)
        act = sb("act", [P, 4, P])
        a3 = sb("a3", [P, M3, P])
        logits = sb("logits", [P, TILES])
        probs = sb("probs", [P, TILES])
        table_warm = sb("table_warm", [P, 1])

        with ExitStack() as start:
            with ExitStack() as first:
                wdf_sb = sb("wdf_sb", [P, 2, BOT[3]], where=first)
                idx = sb("idx", [P, TILES, N_CAT], I32, where=first)
                idx_clip = sb("idx_clip", [P, TILES, N_CAT], I32, where=first)
                idx_neg = sb("idx_neg", [P, TILES, N_CAT], I32, where=first)
                base = sb("base", [P, TILES, N_CAT], I32, where=first)
            xb = sb("xb", [P, NZ + HALF, 32], where=start)
            xw = sb("xw", [P, HALF, 2, HALF], where=start)
            xp = sb("xp", [P, NZ, HALF], where=start)
            sb("gap", [P, 2 * M1 * P - 32 * (NZ + HALF) - 2 * HALF * HALF - PAIRS], where=start)
            w1d = sb("w1d", [P, TOP[1]], where=start)
            wd2_sb = sb("wd2_sb", [P, 4, BOT[2]], where=start)
        a1h = sb("a1h", [P, M1, P], F32R)
        a1l = sb("a1l", [P, M1, P], F32R)
        a2h = sb("a2h", [P, M2, P], F32R)
        a2l = sb("a2l", [P, M2, P], F32R)
        xc = act[:].rearrange("p a b -> p (a b)")[0:N_CONT, :]
        wd1_sb = a3[:].rearrange("p a b -> p (a b)")[0:N_CONT, :]
        h1 = pre[:, 0:4, :]
        h2 = pre[:, 4:6, :]

        z4 = s_ij[:].rearrange("p j g -> p (j g)")[:, 0:2 * TOP[4]].rearrange("p (h n) -> p h n", h=2)

        tp = pb("tp", [P, 2, 512])
        gp = pb("gp", [P, 4, 512])
        mp = pb("mp", [P, 2, 512])

        idx_in = sem("idx_in")
        bottom_in = sem("bottom_in")
        small_in = sem("small_in")
        wd2_in = sem("wd2_in")
        w1d_in = sem("w1d_in")
        w1_in = [sem(f"w1_in{c}") for c in range(PAIR_CHUNKS)]
        w4_in = sem("w4_in")
        rows4_in = sem("rows4_in")
        w_in = [sem(f"w_in{n}") for n in range(SPLIT_LOADS)]
        base_made = sem("base_made")
        ident_made = sem("ident_made")
        zeroed = sem("zeroed")
        idx_step = sem("idx_step")
        gathered = [sem(f"gathered{g}") for g in range(NG)]
        bot_ready = sem("bot_ready")
        bot_out = sem("bot_out")
        pre_ready = sem("pre_ready")
        pre_out = sem("pre_out")
        w_hi = sem("w_hi")
        w_lo = sem("w_lo")
        ft_ready = sem("ft_ready")
        zt_hi = sem("zt_hi")
        zt_lo = sem("zt_lo")
        gram_ready = sem("gram_ready")
        ex_half = sem("ex_half")
        ex_done = sem("ex_done")
        xb_ready = sem("xb_ready")
        xw_ready = sem("xw_ready")
        xp_ready = sem("xp_ready")
        pairs_ready = sem("pairs_ready")
        xt_ready = sem("xt_ready")
        l1_ready = sem("l1_ready")
        l1_out = sem("l1_out")
        a1_hi = sem("a1_hi")
        a2_hi = sem("a2_hi")
        a_lo = sem("a_lo")
        l2_ready = sem("l2_ready")
        l3_ready = sem("l3_ready")
        raw_ready = sem("raw_ready")
        turned = sem("turned")
        relu_act = sem("relu_act")
        relu_dve = sem("relu_dve")
        a3_ready = sem("a3_ready")
        l4_ready = sem("l4_ready")
        z4_ready = sem("z4_ready")
        logits_ready = sem("logits_ready")
        probs_ready = sem("probs_ready")
        out_done = sem("out_done")

        def last_turned(h):
            return tp[:, 1, 0:2 * P] if h == 0 else gp[:, 0, 0:2 * P]

        def bias(name, m):
            return sm[:, COLS[name] + m:COLS[name] + m + 1]

        def l1_bank(m):
            return gp[:, m % 5, 0:P] if m % 5 < 4 else mp[:, 0, 0:P]

        def gram_banks(t, r):
            return gp[:, 2 * (r % 2):2 * (r % 2) + 2, :] if t else tp[:, 0:2, :] if r % 3 == 2 else gp[:, 2 * (r % 3):2 * (r % 3) + 2, :]

        def blocks(a, t, r, q):
            n = 2 * Q * NZE
            pairs = gram_banks(t, r)[32 * q:32 * q + NZ, :, 0:2 * n].rearrange("p k (g c) -> p k g c", g=2)
            return pairs[:, :, :, NZE * (Q * a + q):NZE * (Q * a + q) + NZ]

        def sums(r, q):
            return s_ij[32 * q:32 * q + NZ, :, ROUND * r:ROUND * (r + 1)].rearrange("p j (k g) -> p k g j", k=2)

        def zt_features(part, g):
            f0, nf = Z_GROUPS[g]
            return zt[:, :, part, :, f0:f0 + nf].rearrange("p g q f -> p f q g")

        def transposed(g):
            nf = Z_GROUPS[g][1]
            return gp[:, g % 4, 0:nf * P].rearrange("p (f q g) -> p f q g", f=nf, q=Q)

        def zt_dense(part):
            return zt[:, :, part, :, N_CAT].rearrange("p g q -> p q g")

        def dense(t):
            return dense_t[:, t * P:(t + 1) * P].rearrange("p (q g) -> p q g", q=Q)

        def split_weights(n):
            if n < M1:
                return [w[:, n, :] for w in (w2, w2h, w2l)]
            k = 2 * (n - M1)
            return [w[:, k:k + 2, :].rearrange("p k n -> p (k n)") for w in (w3, w3h, w3l)]

        block = ctx.enter_context(nc.Block())

        @block.sync
        def _(sp):
            sp.dma_start(idx[:], cat_idx.rearrange("(t p) c -> p t c", p=P)).then_inc(idx_in, 16)
            sp.dma_start(wd1_sb[:], wd1).then_inc(bottom_in, 16)
            sp.dma_start(xc[:], x_t).then_inc(bottom_in, 16)
            sp.dma_start(sm[:], small).then_inc(small_in, 16)
            sp.dma_start(wd2_sb[:], wd2.rearrange("(k p) n -> p k n", p=P)).then_inc(wd2_in, 16)
            sp.dma_start(wdf_sb[:], wdf.rearrange("(k p) n -> p k n", p=P)).then_inc(wd2_in, 16)

            def load_to_split(n):
                dst = split_weights(n)[0]
                if n < M1:
                    src = wt2[n * P:(n + 1) * P, :]
                else:
                    k = 2 * (n - M1)
                    src = wt3[k * P:(k + 2) * P, :].rearrange("(k p) n -> p k n", p=P)
                    dst = dst.rearrange("p (k n) -> p k n", k=2)
                sp.dma_start(dst, src).then_inc(w_in[n], 16)

            load_to_split(0)
            sp.dma_start(w1d[:], wt1[PAIRS:PAIRS + E, :]).then_inc(w1d_in, 16)
            for n in range(1, M1):
                if n >= 3:
                    sp.wait_ge(w_in[n - 2], 16)
                load_to_split(n)
            for c in range(PAIR_CHUNKS):
                if c < 2:
                    sp.wait_ge(w_in[M1 - 2 + c], 16)
                else:
                    sp.wait_ge(w1_in[0], 16)
                sp.dma_start(w1[0:PC, c, :], wt1[c * PC:(c + 1) * PC, :]).then_inc(w1_in[c], 16)
            sp.wait_ge(gathered[NG - 1], 16 * Z_GROUPS[NG - 1][1])
            for n in range(M1, SPLIT_LOADS):
                load_to_split(n)
            sp.dma_start(w4[:], wt4.rearrange("(k p) n -> p k n", p=P)).then_inc(w4_in, 16)
            sp.dma_start(b4_wo[:].rearrange("p a n -> p (a n)"),
                         bass.AP(tensor=rows4.tensor, offset=rows4.offset, ap=[[0, P], [1, 2 * TOP[4]]])).then_inc(rows4_in, 16)
            for t in range(TILES):
                sp.wait_ge(probs_ready, t + 1)
                sp.dma_start(out[t * P:(t + 1) * P, :], probs[:, t:t + 1]).then_inc(out_done, 16)
            sp.wait_ge(out_done, 16 * TILES)

        @block.gpsimd
        def _(pool):
            pool.iota(base[:], pattern=[[0, TILES], [VOCAB, N_CAT]], base=0, channel_multiplier=0).then_inc(base_made, 1)
            pool.memset(ident[:], 0.0).then_inc(ident_made, 1)
            pool.wait_ge(ident_made, 1)
            pool.affine_select(out=ident[:], in_=ident[:], compare_op=ALU.not_equal, fill=1.0, base=0,
                               pattern=[[-1, P]], channel_multiplier=1).then_inc(ident_made, 1)
            pool.wait_ge(idx_step, 4)
            for t in range(TILES):
                for g, (f0, nf) in enumerate(Z_GROUPS):
                    if t >= 1:
                        pool.wait_ge(ft_ready, NG * (t - 1) + g + 1)
                    for f in range(f0, f0 + nf):
                        pool.indirect_dma_start(
                            out=rows[:, f, :], out_offset=None, in_=emb.rearrange("c v e -> (c v) e"),
                            in_offset=bass.IndirectOffsetOnAxis(ap=row_of[:, t, f:f + 1].bitcast(U32), axis=0),
                        ).then_inc(gathered[g], 16)

        @block.tensor
        def _(pe):
            def bottom():
                pe.wait_ge(bottom_in, 32)
                n = 0
                for m in range(4):
                    at_least(pe, bot_out, n - 1)
                    pe.matmul(mp[:, n % 2, :], wd1_sb[:, m * P:(m + 1) * P], xc[:], start=True, stop=True).then_inc(bot_ready, 1)
                    n += 1
                pe.wait_ge(wd2_in, 32)
                for m in range(2):
                    at_least(pe, bot_out, n - 1)
                    for k in range(4):
                        if m == 0:
                            pe.wait_ge(bot_out, k + 1)
                        last = pe.matmul(mp[:, n % 2, :], wd2_sb[:, k, m * P:(m + 1) * P], h1[:, k, :], start=(k == 0), stop=(k == 3))
                    last.then_inc(bot_ready, 1)
                    n += 1
                for k in range(2):
                    pe.wait_ge(bot_out, 4 + k + 1)
                    last = pe.matmul(mp[:, n % 2, :], wdf_sb[:, k, :], h2[:, k, :], start=(k == 0), stop=(k == 1))
                last.then_inc(bot_ready, 1)

            def keep_warm():
                pe.wait_ge(pre_out, 4)
                for _ in range(2):
                    pe.matmul(mp[:, 1, 0:2 * P], ident[:], dense_t[:, 0:2 * P], start=True, stop=True)

            def dense_products(m):
                if m == 0:
                    pe.wait_ge(bot_out, 7)
                elif m >= 2:
                    pe.wait_ge(pre_out, m - 1)
                pe.matmul(mp[:, (m + 1) % 2, :], w1d[:, m * P:(m + 1) * P], dense_t[:], start=True, stop=True).then_inc(pre_ready, 1)

            def transpose_feature(t, f):
                g, n = f // ZG, f % ZG
                if n == 0:
                    pe.wait_ge(gathered[g], 16 * Z_GROUPS[g][1] * (t + 1))
                    if g >= 4:
                        pe.wait_ge(zt_lo, (1 + NG) * t + 1 + g - 3)
                    elif t >= 1:
                        pe.wait_ge(l1_out, M1 * (t - 1) + min(6 + g, M1))
                feature = pe.transpose(gp[:, g % 4, n * P:(n + 1) * P], rows[:, f, :], ident[:])
                if n == Z_GROUPS[g][1] - 1:
                    feature.then_inc(ft_ready, 1)

            def gram(t, g):
                r, k = g // ROUND, g % ROUND
                if g == 0:
                    pe.wait_ge(zt_lo, (1 + NG) * (t + 1))
                before = r - (2 if t else 3)
                if k == 0 and before >= 0:
                    pe.wait_ge(ex_done, ROUNDS * t + before + 1)
                n = 2 * Q * NZE
                last = pe.matmul(gram_banks(t, r)[0:GRAM_M, k // 2, n * (k % 2):n * (k % 2 + 1)],
                                 zt[:, g, 0, :, :].rearrange("p q f -> p (q f)")[:, 0:GRAM_M], zt[:, g, :, :, 0:NZE], start=True, stop=True)
                if k == ROUND - 1:
                    last.then_inc(gram_ready, 1)

            def transpose_pairs(t):
                at_least(pe, relu_act, 4 * t)
                for c in range(PAIR_CHUNKS):
                    pe.wait_ge(xp_ready, 2 * t + (1 if IC * (c + 1) <= NZ - HALF else 2))
                    src = xp[:, IC * c:IC * (c + 1), :].rearrange("p i d -> p (i d)")
                    last = pe.transpose(tp[0:PC, 0, c * P:(c + 1) * P], src, ident[:])
                last.then_inc(pairs_ready, 1)

            def layer_1(t, m):
                if m == 4 and t == 0:
                    pe.wait_ge(pre_out, M1)
                if m >= 5:
                    pe.wait_ge(l1_out, M1 * t + m - 4)
                for k in range(PAIR_CHUNKS):
                    if m == 0:
                        pe.wait_ge(xt_ready, PAIR_CHUNKS * t + k + 1)
                    last = pe.matmul(l1_bank(m), w1[0:PC, k, m * P:(m + 1) * P], xt[0:PC, k, :], start=(k == 0), stop=(k == PAIR_CHUNKS - 1))
                last.then_inc(l1_ready, 1)

            def product(o, ah, al, wh, wl, k, n, cols, t, lo):
                pe.matmul(o, ah[:, k, :], wh[:, k, cols], start=(k == 0), stop=False)
                next_steps(t)
                pe.matmul(o, ah[:, k, :], wl[:, k, cols], start=False, stop=False)
                next_steps(t)
                if lo > 0:
                    pe.wait_ge(a_lo, lo)
                last = pe.matmul(o, al[:, k, :], wh[:, k, cols], start=False, stop=(k == n - 1))
                if k < n - 1:
                    next_steps(t)
                return last

            def turn(t, h):
                pe.wait_ge(raw_ready, 3 * t + h + 1)
                if h == 1:
                    pe.wait_ge(relu_act, 4 * t + 2)
                    pe.wait_ge(relu_dve, 4 * t + 2)
                for c in range(4):
                    o = tp[:, c // 2, (c % 2) * P:(c % 2 + 1) * P] if h < 2 else tp[:, 1, c * P:(c + 1) * P]
                    last = pe.transpose(o, raw[:, h % 2, c * P:(c + 1) * P], ident[:])
                last.then_inc(turned, 1)

            slot = [0] * TILES

            def next_steps(t):
                for step, steps, (first, last) in ((transpose_feature, N_CAT, FEATURE_SLOTS[t]), (gram, GROUPS, GRAM_SLOTS[t])):
                    n, slots = slot[t] - first, last - first
                    if 0 <= n < slots and t + 1 < TILES:
                        for s in range(n * steps // slots, (n + 1) * steps // slots):
                            step(t + 1, s)
                slot[t] += 1

            def layer_2(t):
                if t == 0:
                    pe.wait_ge(w_lo, M1)
                for h in range(2):
                    if h == 0:
                        pe.wait_ge(l1_out, M1 * t + 5)
                    else:
                        at_least(pe, z4_ready, t)
                    for k in range(M1):
                        lo = 0
                        if h == 0 and k % 2 == 0:
                            pe.wait_ge(a1_hi, 4 * t + k // 2 + 1)
                            lo = 8 * t + k // 2 + 1
                        if h == 1 and k == 4:
                            turn(t, 0)
                        last = product(mp[:, h, :], a1h, a1l, w2h, w2l, k, M1, slice(h * HALF2, (h + 1) * HALF2), t, lo)
                    last.then_inc(l2_ready, 1)

            def layer_3(t):
                if t == 0:
                    pe.wait_ge(w_lo, SPLIT_LOADS)
                for k in range(M2):
                    if k == (2 if t else 1):
                        turn(t, 1)
                    if k == 7 and 0 < t < TILES - 1:
                        transpose_pairs(t + 1)
                    lo = 0
                    if k % 2 == 0:
                        pe.wait_ge(a2_hi, 4 * t + k // 2 + 1)
                        lo = 8 * t + 4 + k // 2 + 1
                    last = product(mp[:, 0, :], a2h, a2l, w3h, w3l, k, M2, slice(0, TOP[3]), t, lo)
                last.then_inc(l3_ready, 1)

            def layer_4(t):
                if t == 0:
                    pe.wait_ge(w4_in, 16)
                for k in range(M3):
                    pe.wait_ge(a3_ready, M3 * t + k + 1)
                    last = pe.matmul(mp[:, 1, 0:TOP[4]], a3[:, k, :], w4[:, k, :], start=(k == 0), stop=(k == M3 - 1))
                last.then_inc(l4_ready, 1)

            bottom()
            pe.wait_ge(ident_made, 2)
            pe.wait_ge(w1d_in, 16)
            for f in range(4 * ZG):
                transpose_feature(0, f)
            for m in range(4):
                dense_products(m)
            for f in range(4 * ZG, N_CAT):
                transpose_feature(0, f)
            keep_warm()
            for g in range(GROUPS):
                gram(0, g)
            for m in range(4, M1):
                dense_products(m)
            transpose_pairs(0)
            for c in range(PAIR_CHUNKS):
                pe.wait_ge(w1_in[c], 16)
            for t in range(TILES):
                for m in range(M1):
                    if t >= 2 and m == 2:
                        turn(t - 1, 2)
                    if t >= 2 and m == 5:
                        layer_4(t - 1)
                    layer_1(t, m)
                layer_2(t)
                layer_3(t)
                if t == 0:
                    turn(0, 2)
                    transpose_pairs(1)
                    layer_4(0)
            for h in range(2):
                pe.wait_ge(raw_ready, 3 * (TILES - 1) + 2 + h + 1)
                for c in range(2):
                    last = pe.transpose(last_turned(h)[:, c * P:(c + 1) * P], raw[:, 0, (2 * h + c) * P:(2 * h + c + 1) * P], ident[:])
                last.then_inc(turned, 1)
            layer_4(TILES - 1)

        @block.scalar
        def _(sc):
            def split_hi(n):
                weights, high, _ = split_weights(n)
                sc.wait_ge(w_in[n], 16)
                sc.copy(high, weights).then_inc(w_hi, 1)

            def bottom_out(n):
                name, m, dst = (("bd1", n, h1[:, n, :]) if n < 4 else ("bd2", n - 4, h2[:, n - 4, :]) if n < 6 else ("bdf", 0, dense_t[:]))
                sc.wait_ge(bot_ready, n + 1)
                sc.activation(dst, mp[:, n % 2, :], ACT.Relu, bias=bias(name, m)).then_inc(bot_out, 1)

            def dense_products_out(m):
                sc.wait_ge(pre_ready, m + 1)
                sc.activation(pre[:, m, :], mp[:, (m + 1) % 2, :], ACT.Identity, bias=bias("bt1", m)).then_inc(pre_out, 1)

            def dense_feature(t):
                sc.wait_ge(bot_out, 7)
                at_least(sc, gram_ready, ROUNDS * t)
                sc.copy(zt_dense(0), dense(t)).then_inc(zt_hi, 1)

            def features(t, g):
                sc.wait_ge(ft_ready, NG * t + g + 1)
                sc.copy(zt_features(0, g), transposed(g)).then_inc(zt_hi, 1)

            def gram(t, r):
                if r == 0:
                    at_least(sc, xb_ready, 2 * t)
                    at_least(sc, logits_ready, t - 1)
                sc.wait_ge(gram_ready, ROUNDS * t + r + 1)
                for q in range(Q):
                    sc.activation(sums(r, q), blocks(0, t, r, q), ACT.Copy, scale=0.5).then_inc(ex_half, 1)

            def wrap_columns(t):
                sc.wait_ge(xb_ready, 2 * t + 1)
                sc.copy(xw[:, :, 0, :], xb[:, NZ - HALF:NZ, NZ - HALF:NZ])
                sc.copy(xw[:, :, 1, :], xb[:, NZ - HALF:NZ, 0:HALF]).then_inc(xw_ready, 1)

            def relu_half(t, h):
                sc.wait_ge(turned, 3 * t + h + 1)
                sc.wait_ge(a_lo, 8 * t + 4 + 2 * h)
                for c in range(2):
                    sc.activation(act[:, c, :], tp[:, 0, c * P:(c + 1) * P], ACT.Relu, bias=bias("bt2", 4 * h + c)).then_inc(relu_act, 1)

            def half_2_hi(t, h, n):
                k = 4 * h + 2 * n
                sc.wait_ge((relu_act, relu_dve)[n], 4 * t + 2 * h + 2)
                sc.copy(a2h[:, k:k + 2, :], act[:, 2 * n:2 * n + 2, :]).then_inc(a2_hi, 1)

            def copy_sums(t, h, bank, ready, n):
                sc.wait_ge(ready, n)
                sc.copy(raw[:, h % 2, :], mp[:, bank, :]).then_inc(raw_ready, 1)

            def relu_3(t):
                sc.wait_ge(turned, 3 * t + 3)
                for c in range(M3):
                    sc.activation(a3[:, c, :], tp[:, 1, c * P:(c + 1) * P], ACT.Relu, bias=bias("bt3", c)).then_inc(a3_ready, 1)

            def sigmoid(t):
                sc.wait_ge(logits_ready, t + 1)
                sc.activation(probs[:, t:t + 1], logits[:, t:t + 1], ACT.Sigmoid, bias=bias("bo", 0)).then_inc(probs_ready, 1)

            sc.wait_ge(ident_made, 2)
            sc.activation(table_warm[:], ident[:, 0:1], ACT.Sigmoid)
            sc.wait_ge(small_in, 16)
            for n in range(4):
                bottom_out(n)
            split_hi(0)
            split_hi(1)
            bottom_out(4)
            split_hi(2)
            split_hi(3)
            bottom_out(5)
            split_hi(4)
            bottom_out(6)
            dense_feature(0)
            for g in range(4):
                features(0, g)
            split_hi(5)
            for m in range(4):
                dense_products_out(m)
                if m % 2:
                    split_hi(6 + m // 2)
            for g in range(4, NG):
                features(0, g)
            sc.wait_ge(zeroed, 1)
            for r in range(ROUNDS):
                gram(0, r)
            dense_products_out(4)
            dense_products_out(5)
            wrap_columns(0)
            dense_products_out(6)
            dense_products_out(7)
            for n in range(M1, SPLIT_LOADS):
                split_hi(n)

            for t in range(TILES):
                more = t + 1 < TILES
                for n in range(M1 // 2):
                    sc.wait_ge(l1_out, M1 * t + 2 * n + 2)
                    sc.activation(a1h[:, 2 * n:2 * n + 2, :], act[:, 2 * (n % 2):2 * (n % 2) + 2, :], ACT.Relu).then_inc(a1_hi, 1)
                    if t >= 2 and n == 0:
                        relu_3(t - 1)
                if more:
                    dense_feature(t + 1)
                if t >= 1:
                    sigmoid(t - 1)
                if more:
                    for g in range(NG):
                        if t == 0 and g == 5:
                            copy_sums(0, 0, 0, l2_ready, 1)
                        features(t + 1, g)
                for r in range(ROUNDS):
                    if t >= 1 and r == 1:
                        copy_sums(t, 0, 0, l2_ready, 2 * t + 1)
                    if r == RELU_ROUND[t]:
                        relu_half(t, 0)
                    if 0 < r - RELU_ROUND[t] < 3:
                        half_2_hi(t, 0, r - RELU_ROUND[t] - 1)
                    if t == 0 and r == 3:
                        copy_sums(0, 1, 1, l2_ready, 2)
                    if t == 0 and r == 5:
                        relu_half(0, 1)
                    if t == 0 and r == 6:
                        half_2_hi(0, 1, 0)
                        half_2_hi(0, 1, 1)
                    if more:
                        gram(t + 1, r)
                if t >= 1:
                    copy_sums(t, 1, 1, l2_ready, 2 * t + 2)
                    relu_half(t, 1)
                    half_2_hi(t, 1, 0)
                    half_2_hi(t, 1, 1)
                if more and t >= 1:
                    wrap_columns(t + 1)
                if more:
                    copy_sums(t, 2, 0, l3_ready, t + 1)
                if t == 0:
                    wrap_columns(1)
                    relu_3(0)
            t = TILES - 1
            sc.wait_ge(l3_ready, t + 1)
            for h in range(2):
                sc.copy(raw[:, 0, 2 * h * P:2 * (h + 1) * P], mp[:, 0, 2 * h * P:2 * (h + 1) * P]).then_inc(raw_ready, 1)
            for h in range(2):
                sc.wait_ge(turned, 3 * t + 2 + h + 1)
                for c in range(2):
                    sc.activation(a3[:, 2 * h + c, :], last_turned(h)[:, c * P:(c + 1) * P], ACT.Relu, bias=bias("bt3", 2 * h + c)).then_inc(a3_ready, 1)
            sigmoid(t)

        @block.vector
        def _(ve):
            ve.wait_ge(idx_in, 16)
            ve.tensor_scalar(idx_clip[:], idx[:], float(-VOCAB), float(VOCAB - 1), ALU.max, ALU.min).then_inc(idx_step, 1)
            ve.wait_ge(idx_step, 1)
            ve.tensor_scalar(idx_neg[:], idx_clip[:], 0.0, float(VOCAB), ALU.is_lt, ALU.mult).then_inc(idx_step, 1)
            ve.wait_ge(idx_step, 2)
            ve.tensor_tensor(idx[:], idx_clip[:], idx_neg[:], ALU.add).then_inc(idx_step, 1)
            ve.wait_ge(idx_step, 3)
            ve.wait_ge(base_made, 1)
            ve.tensor_tensor(row_of[:], idx[:], base[:], ALU.add).then_inc(idx_step, 1)
            ve.memset(s_ij[:], 0.0).then_inc(zeroed, 1)
            ve.memset(zt[:, :, :, :, NZ:32].bitcast(F32), 0.0).then_inc(zeroed, 1)

            def split_lo(n):
                weights, high, low = split_weights(n)
                ve.wait_ge(w_hi, n + 1)
                ve.tensor_tensor(low, weights, high.bitcast(F32), ALU.subtract).then_inc(w_lo, 1)

            def dense_feature(t):
                ve.wait_ge(zt_hi, (1 + NG) * t + 1)
                ve.tensor_tensor(zt_dense(1), dense(t), zt_dense(0).bitcast(F32), ALU.subtract).then_inc(zt_lo, 1)

            def features(t, g):
                ve.wait_ge(zt_hi, (1 + NG) * t + g + 2)
                ve.tensor_tensor(zt_features(1, g), transposed(g), zt_features(0, g).bitcast(F32), ALU.subtract).then_inc(zt_lo, 1)

            def gram(t, r):
                ve.wait_ge(gram_ready, ROUNDS * t + r + 1)
                for q in range(Q):
                    ve.wait_ge(ex_half, Q * (ROUNDS * t + r) + q + 1)
                    last = ve.tensor_tensor(sums(r, q), sums(r, q), blocks(1, t, r, q), ALU.add)
                last.then_inc(ex_done, 1)

            def turn_rows(t):
                at_least(ve, l2_ready, 2 * t)
                ve.wait_ge(ex_done, ROUNDS * (t + 1))
                ve.transpose(xb[:, 0:NZ, :].rearrange("p j i -> p (j i)"), s_ij[:].rearrange("p j g -> p (j g)")).then_inc(xb_ready, 1)

            def gather_pairs(t):
                ve.transpose(xb[:, NZ:NZ + HALF, :].rearrange("p j i -> p (j i)"), s_ij[:, 0:HALF, :].rearrange("p j g -> p (j g)")).then_inc(xb_ready, 1)
                ve.wait_ge(xb_ready, 2 * (t + 1))

                def diagonals(x, at, n, row, step):
                    flat = x[:].rearrange("p a b -> p (a b)") if x is xb else x[:].rearrange("p a b c -> p (a b c)")
                    return bass.AP(tensor=flat.tensor, offset=flat.offset + at, ap=[list(flat.ap[0]), [row, n], [step, HALF]])

                n = NZ - HALF
                ve.tensor_tensor(xp[:, 0:n, :], diagonals(xb, 32, n, 33, 32), diagonals(xb, 1, n, 33, 1), ALU.add).then_inc(xp_ready, 1)
                ve.wait_ge(xw_ready, t + 1)
                ve.tensor_tensor(xp[:, n:NZ, :], diagonals(xb, 33 * n + 32, HALF, 33, 32), diagonals(xw, 1, HALF, 2 * HALF + 1, 1), ALU.add).then_inc(xp_ready, 1)

            def pairs_out(t):
                ve.wait_ge(pairs_ready, t + 1)
                for c in range(PAIR_CHUNKS):
                    ve.tensor_copy(xt[0:PC, c, :], tp[0:PC, 0, c * P:(c + 1) * P]).then_inc(xt_ready, 1)

            def layer_1_out(t, m):
                ve.wait_ge(l1_ready, M1 * t + m + 1)
                at_least(ve, a_lo, 8 * t + m // 2 - 1)
                ve.tensor_tensor(act[:, m % 4, :], l1_bank(m), pre[:, m, t * P:(t + 1) * P], ALU.add).then_inc(l1_out, 1)

            def layer_1_lo(t, n):
                ve.wait_ge(a1_hi, 4 * t + n + 1)
                ve.scalar_tensor_tensor(out=a1l[:, 2 * n:2 * n + 2, :], in0=act[:, 2 * (n % 2):2 * (n % 2) + 2, :], scalar=0.0,
                                        in1=a1h[:, 2 * n:2 * n + 2, :].bitcast(F32), op0=ALU.max, op1=ALU.subtract).then_inc(a_lo, 1)

            def relu_half(t, h):
                ve.wait_ge(turned, 3 * t + h + 1)
                ve.wait_ge(a_lo, 8 * t + 4 + 2 * h)
                for c in range(2):
                    ve.tensor_scalar(act[:, 2 + c, :], tp[:, 1, c * P:(c + 1) * P], bias("bt2", 4 * h + 2 + c), 0.0,
                                     ALU.add, ALU.max).then_inc(relu_dve, 1)

            def half_2_lo(t, h, n):
                k = 4 * h + 2 * n
                ve.wait_ge(a2_hi, 4 * t + 2 * h + n + 1)
                ve.tensor_tensor(a2l[:, k:k + 2, :], act[:, 2 * n:2 * n + 2, :], a2h[:, k:k + 2, :].bitcast(F32), ALU.subtract).then_inc(a_lo, 1)

            def last_layers(t):
                ve.wait_ge(l4_ready, t + 1)
                ve.tensor_tensor(z4[:, 0, :], mp[:, 1, 0:TOP[4]], b4_wo[:, 0, :], ALU.add).then_inc(z4_ready, 1)
                ve.wait_ge(z4_ready, t + 1)
                ve.scalar_tensor_tensor(out=z4[:, 1, :], in0=z4[:, 0, :], scalar=0.0, in1=b4_wo[:, 1, :], op0=ALU.max,
                                        op1=ALU.mult, accum_out=logits[:, t:t + 1]).then_inc(logits_ready, 1)

            for n in range(5):
                split_lo(n)
            dense_feature(0)
            for g in range(4):
                features(0, g)
            for n in range(5, M1):
                split_lo(n)
            for g in range(4, NG):
                features(0, g)
            for r in range(ROUNDS):
                gram(0, r)
            turn_rows(0)
            gather_pairs(0)
            ve.wait_ge(rows4_in, 16)
            for t in range(TILES):
                more = t + 1 < TILES
                pairs_out(t)
                for n in range(2):
                    if t == 0:
                        split_lo(M1 + n)
                    layer_1_out(t, n)
                for n in range(M1 // 2):
                    if n < M1 // 2 - 1:
                        layer_1_out(t, 2 * n + 2)
                        layer_1_out(t, 2 * n + 3)
                    layer_1_lo(t, n)
                    if t >= 1 and n == 1:
                        last_layers(t - 1)
                if t == 0:
                    split_lo(M1 + 2)
                    split_lo(M1 + 3)
                if more:
                    dense_feature(t + 1)
                    for g in range(NG):
                        features(t + 1, g)
                for r in range(ROUNDS):
                    if r == RELU_ROUND[t]:
                        relu_half(t, 0)
                    if t == 0 and r == 5:
                        relu_half(0, 1)
                    if more:
                        gram(t + 1, r)
                    if 0 < r - RELU_ROUND[t] < 3:
                        half_2_lo(t, 0, r - RELU_ROUND[t] - 1)
                    if t == 0 and r == 6:
                        half_2_lo(0, 1, 0)
                        half_2_lo(0, 1, 1)
                if more:
                    turn_rows(t + 1)
                if t >= 1:
                    relu_half(t, 1)
                    half_2_lo(t, 1, 0)
                    half_2_lo(t, 1, 1)
                if more:
                    gather_pairs(t + 1)
            last_layers(TILES - 1)


def pair_rows():
    rows = []
    for i in range(NZ):
        for d in range(1, HALF + 1):
            lo, hi = sorted((i, (i + d) % NZ))
            rows.append(lo * (2 * NZ - lo - 1) // 2 + hi - lo - 1)
    return rows


def kernel(**inputs):
    import numpy as np
    import concourse.bacc as bacc
    from concourse.bass_utils import run_bass_kernel_spmd as run

    a = {k.replace("L0_rec_", ""): np.asarray(v) for k, v in inputs.items()}
    small = np.concatenate([np.broadcast_to(a[n], (P, 1)) if n == "bo" else a[n].reshape(-1, P).T for n in COLS], axis=1)
    order = pair_rows() + list(range(PAIRS, PAIRS + E))
    laid_out = {
        "x_t": a["r_dense_x"].T, "cat_idx": a["r_cat_idx"], "emb": a["emb_table"], "small": small,
        "rows4": np.concatenate([a["bt4"].reshape(1, -1), a["Wo"].reshape(1, -1)], axis=1), "wd1": a["Wd1"], "wd2": a["Wd2"], "wdf": a["Wdf"],
        "wt1": a["Wt1"][order], "wt2": a["Wt2"], "wt3": a["Wt3"], "wt4": a["Wt4"],
    }
    nc = bacc.Bacc("TRN2", target_bir_lowering=False, num_devices=1)
    arrays, args = {}, []
    for name, x in laid_out.items():
        x = np.ascontiguousarray(x)
        arrays[f"in_{name}"] = x
        args.append(nc.dram_tensor(f"in_{name}", x.shape, mybir.dt.from_np(x.dtype), kind="ExternalInput").ap())
    args.append(nc.dram_tensor("out_0", (BATCH, 1), F32, kind="ExternalOutput").ap())
    build(nc, *args)
    r = run(nc, [arrays], core_ids=[0])
    return r.results[0]["out_0"]
```
